# Optimizing a Trainium2 kernel written in Bass

```python
import numpy as np
import jax
import jax.numpy as jnp

def _softmax(x, axis=-1):
    return jax.nn.softmax(x, axis=axis)

def _gelu(x):
    return jax.nn.gelu(x, approximate=True)

def _silu(x):
    return jax.nn.silu(x)

def _sigmoid(x):
    return jax.nn.sigmoid(x)

def _layernorm(x, axis=-1, eps=1e-05):
    m = jnp.mean(x, axis=axis, keepdims=True)
    v = jnp.var(x, axis=axis, keepdims=True)
    return (x - m) / jnp.sqrt(v + eps)

def _scatter_add(tgt, idx, src, axis=0):
    return tgt.at[idx].add(src)

def _segment_sum(src, seg, n):
    return jax.ops.segment_sum(src, seg, n)
kernel_name = 'mk_macaron_d1_jaxref_r8_9d1ecd'

def setup_inputs(seed: int=0):
    np.random.seed(seed)
    _w = jnp.asarray

    def _L0_attn_setup():
        import jax, jax.numpy as jnp
        import numpy as np
        B, T, D = (1, 256, 128)
        H, DH, DV, DF = (16, 64, 64, 512)
        EPS_LN = 1e-05
        EPS_DEN = 1e-06

        def _layernorm(x, g, b):
            m = jnp.mean(x, axis=-1, keepdims=True)
            v = jnp.mean((x - m) ** 2, axis=-1, keepdims=True)
            return (x - m) / jnp.sqrt(v + EPS_LN) * g + b

        def _phi(x):
            return jax.nn.elu(x) + 1.0

        def _linear_attention(x, Wq, Wk, Wv, Wo):
            b, t, d = x.shape
            Q = _phi((x @ Wq).reshape(b, t, H, DH)).transpose(0, 2, 1, 3)
            K = _phi((x @ Wk).reshape(b, t, H, DH)).transpose(0, 2, 1, 3)
            V = (x @ Wv).reshape(b, t, H, DV).transpose(0, 2, 1, 3)
            KV = jnp.einsum('bhti,bhtj->bhtij', K, V)
            S = jnp.cumsum(KV, axis=2)
            z = jnp.cumsum(K, axis=2)
            num = jnp.einsum('bhti,bhtij->bhtj', Q, S)
            den = jnp.maximum(jnp.einsum('bhti,bhti->bht', Q, z), EPS_DEN)[..., None]
            out = (num / den).transpose(0, 2, 1, 3).reshape(b, t, H * DV)
            return out @ Wo
        key = jax.random.key(seed)
        ks = jax.random.split(key, 8)
        s = 0.02
        return {'x': jax.random.normal(ks[0], (B, T, D), dtype=jnp.float32), 'ln1_g': jnp.ones((D,), jnp.float32), 'ln1_b': jnp.zeros((D,), jnp.float32), 'Wq': jax.random.normal(ks[1], (D, H * DH), jnp.float32) * s, 'Wk': jax.random.normal(ks[2], (D, H * DH), jnp.float32) * s, 'Wv': jax.random.normal(ks[3], (D, H * DV), jnp.float32) * s, 'Wo': jax.random.normal(ks[4], (H * DV, D), jnp.float32) * s, 'ln2_g': jnp.ones((D,), jnp.float32), 'ln2_b': jnp.zeros((D,), jnp.float32), 'Wf1': jax.random.normal(ks[5], (D, DF), jnp.float32) * s, 'Wf2': jax.random.normal(ks[6], (DF, D), jnp.float32) * s}
    _L0_attn_in = _L0_attn_setup()

    def _L0_ffn_setup():
        import jax, jax.numpy as jnp
        import numpy as np
        B, T, D, E, H, K = (2, 256, 128, 8, 512, 2)
        key = jax.random.key(seed)
        ks = jax.random.split(key, 8)
        s = 0.02
        return {'x': jax.random.normal(ks[0], (B, T, D), jnp.float32), 'rw1': jax.random.normal(ks[1], (D, D), jnp.float32) * s, 'rb1': jnp.zeros((D,), jnp.float32), 'rw2': jax.random.normal(ks[2], (D, E), jnp.float32) * s, 'rb2': jnp.zeros((E,), jnp.float32), 'we1': jax.random.normal(ks[3], (E, D, H), jnp.float32) * s, 'be1': jnp.zeros((E, H), jnp.float32), 'we2': jax.random.normal(ks[4], (E, H, D), jnp.float32) * s, 'be2': jnp.zeros((E, D), jnp.float32)}
    _L0_ffn_in = _L0_ffn_setup()
    _d = {'L0_attn_x': _L0_attn_in['x'], 'L0_attn_ln1_g': _L0_attn_in['ln1_g'], 'L0_attn_ln1_b': _L0_attn_in['ln1_b'], 'L0_attn_Wq': _L0_attn_in['Wq'], 'L0_attn_Wk': _L0_attn_in['Wk'], 'L0_attn_Wv': _L0_attn_in['Wv'], 'L0_attn_Wo': _L0_attn_in['Wo'], 'L0_attn_ln2_g': _L0_attn_in['ln2_g'], 'L0_attn_ln2_b': _L0_attn_in['ln2_b'], 'L0_attn_Wf1': _L0_attn_in['Wf1'], 'L0_attn_Wf2': _L0_attn_in['Wf2'], 'L0_ffn_rw1': _L0_ffn_in['rw1'], 'L0_ffn_rb1': _L0_ffn_in['rb1'], 'L0_ffn_rw2': _L0_ffn_in['rw2'], 'L0_ffn_rb2': _L0_ffn_in['rb2'], 'L0_ffn_we1': _L0_ffn_in['we1'], 'L0_ffn_be1': _L0_ffn_in['be1'], 'L0_ffn_we2': _L0_ffn_in['we2'], 'L0_ffn_be2': _L0_ffn_in['be2']}
    _x0 = _d['L0_attn_x']
    _d['L0_attn_x'] = jax.random.normal(jax.random.fold_in(jax.random.key(seed), 1), (32, 256, 128), dtype=_x0.dtype)
    del _x0
    return _d

def reference(L0_attn_x, L0_attn_ln1_g, L0_attn_ln1_b, L0_attn_Wq, L0_attn_Wk, L0_attn_Wv, L0_attn_Wo, L0_attn_ln2_g, L0_attn_ln2_b, L0_attn_Wf1, L0_attn_Wf2, L0_ffn_rw1, L0_ffn_rb1, L0_ffn_rw2, L0_ffn_rb2, L0_ffn_we1, L0_ffn_be1, L0_ffn_we2, L0_ffn_be2):

    def _L0_attn_ref(x, ln1_g, ln1_b, Wq, Wk, Wv, Wo, ln2_g, ln2_b, Wf1, Wf2):
        import jax, jax.numpy as jnp
        import numpy as np
        B, T, D = (1, 256, 128)
        H, DH, DV, DF = (16, 64, 64, 512)
        EPS_LN = 1e-05
        EPS_DEN = 1e-06

        def _layernorm(x, g, b):
            m = jnp.mean(x, axis=-1, keepdims=True)
            v = jnp.mean((x - m) ** 2, axis=-1, keepdims=True)
            return (x - m) / jnp.sqrt(v + EPS_LN) * g + b

        def _phi(x):
            return jax.nn.elu(x) + 1.0

        def _linear_attention(x, Wq, Wk, Wv, Wo):
            b, t, d = x.shape
            Q = _phi((x @ Wq).reshape(b, t, H, DH)).transpose(0, 2, 1, 3)
            K = _phi((x @ Wk).reshape(b, t, H, DH)).transpose(0, 2, 1, 3)
            V = (x @ Wv).reshape(b, t, H, DV).transpose(0, 2, 1, 3)
            KV = jnp.einsum('bhti,bhtj->bhtij', K, V)
            S = jnp.cumsum(KV, axis=2)
            z = jnp.cumsum(K, axis=2)
            num = jnp.einsum('bhti,bhtij->bhtj', Q, S)
            den = jnp.maximum(jnp.einsum('bhti,bhti->bht', Q, z), EPS_DEN)[..., None]
            out = (num / den).transpose(0, 2, 1, 3).reshape(b, t, H * DV)
            return out @ Wo
        x = x + _linear_attention(_layernorm(x, ln1_g, ln1_b), Wq, Wk, Wv, Wo)
        h = _layernorm(x, ln2_g, ln2_b)
        x = x + jax.nn.gelu(h @ Wf1, approximate=False) @ Wf2
        return x

    def _L0_ffn_ref(x, rw1, rb1, rw2, rb2, we1, be1, we2, be2):
        import jax, jax.numpy as jnp
        import numpy as np
        B, T, D, E, H, K = (2, 256, 128, 8, 512, 2)
        b, t, d = x.shape
        xt = x.reshape(b * t, d)
        n = xt.shape[0]
        logits = jax.nn.silu(xt @ rw1 + rb1) @ rw2 + rb2
        _, idx = jax.lax.top_k(logits, K)
        mask = jnp.zeros((n, E), bool).at[jnp.arange(n)[:, None], idx].set(True)
        w = jax.nn.softmax(jnp.where(mask, logits, -jnp.inf), axis=1)
        h = jax.nn.silu(jnp.einsum('nd,edh->enh', xt, we1) + be1[:, None, :])
        eo = jnp.einsum('enh,ehd->end', h, we2) + be2[:, None, :]
        y = xt + jnp.einsum('ne,end->nd', w, eo)
        return y.reshape(b, t, d)
    x = L0_attn_x
    x = x + 0.5 * _L0_ffn_ref(_layernorm(x, axis=-1), L0_ffn_rw1, L0_ffn_rb1, L0_ffn_rw2, L0_ffn_rb2, L0_ffn_we1, L0_ffn_be1, L0_ffn_we2, L0_ffn_be2)
    x = x + _L0_attn_ref(_layernorm(x, axis=-1), L0_attn_ln1_g, L0_attn_ln1_b, L0_attn_Wq, L0_attn_Wk, L0_attn_Wv, L0_attn_Wo, L0_attn_ln2_g, L0_attn_ln2_b, L0_attn_Wf1, L0_attn_Wf2)
    x = x + 0.5 * _L0_ffn_ref(_layernorm(x, axis=-1), L0_ffn_rw1, L0_ffn_rb1, L0_ffn_rw2, L0_ffn_rb2, L0_ffn_we1, L0_ffn_be1, L0_ffn_we2, L0_ffn_be2)
    return x

_drawn_inputs = setup_inputs


def setup_inputs(seed=0):
    import zlib

    import numpy as np

    out = dict(_drawn_inputs(seed))
    spreads = {'L0_attn_ln1_g': (1.0, 0.6),
     'L0_attn_ln1_b': (0.0, 0.8),
     'L0_attn_ln2_g': (1.0, 0.6),
     'L0_attn_ln2_b': (0.0, 2.0),
     'L0_ffn_rb1': (0.0, 0.417),
     'L0_ffn_rb2': (0.0, 0.1),
     'L0_ffn_be1': (0.0, 0.8),
     'L0_ffn_be2': (0.0, 0.1)}
    factors = {'L0_attn_Wq': 8.0,
     'L0_attn_Wk': 8.0,
     'L0_attn_Wv': 5.082,
     'L0_attn_Wo': 5.152,
     'L0_ffn_we1': 3.095,
     'L0_ffn_we2': 2.777}
    for name, (base, spread) in spreads.items():
        noise = np.random.default_rng([zlib.crc32(name.encode()), seed]).standard_normal(out[name].shape)
        drawn = base * np.exp(spread * noise) if base else spread * noise
        out[name] = jnp.asarray(drawn.astype(out[name].dtype))
    for name, factor in factors.items():
        out[name] = (out[name] * factor).astype(out[name].dtype)
    return out
```

```python
from contextlib import ExitStack

import concourse.bass as bass
from concourse import mybir

FP32 = mybir.dt.float32
FP32R = mybir.dt.float32r
BF16 = mybir.dt.bfloat16
ALU = mybir.AluOpType
ACT = mybir.ActivationFunctionType
AXIS_X = mybir.AxisListType.X

P = 128
D = 128
E = 8
HID = 512
HC = HID // P
TILE = 512
TQ = TILE // P
EPS_LN = 1e-5
EPS_DEN = 1e-6
UNROLL = 2
AHEAD = 4
RS = 17
RAW = 4
SPLITS = 3

BT = 256
AH = 1024

ROW_BE1, ROW_BE2, ROW_RB1, ROW_G1, ROW_B1, ROW_G2, ROW_B2, ROWS = 0, 32, 40, 41, 42, 43, 44, 45


def load_expert(nc, sp, k, e, s):
    sp.dma_start(k.raw1[:, e % RAW, :], k.we1[e]).then_inc(s, 16)
    sp.dma_start(k.raw2[:, e % RAW, :, :], k.we2[e].rearrange("(c p) d -> p c d", p=P)).then_inc(s, 16)


class Kept:
    pass


def ffn_phase(nc, k, name, x_in=None, loads=None, out=None):
    TILES = k.tiles
    CH = E * HC
    with ExitStack() as ctx:
        def sb(n, shape, dt=FP32):
            return ctx.enter_context(nc.sbuf_tensor(f"{name}_{n}", shape, dt))

        def ps(n):
            return ctx.enter_context(nc.psum_tensor(f"{name}_{n}_ps", [P, 512], FP32))

        def sem(n):
            return ctx.enter_context(nc.semaphore(f"{name}_{n}_sem"))

        if loads:
            rawr = sb("rawr", [P, D])
            rows = sb("rows", [ROWS, P])
        w1_hi, w1_lo = sb("w1_hi", [P, E, HID], FP32R), sb("w1_lo", [P, E, HID], FP32R)
        w2_hi, w2_lo = sb("w2_hi", [P, E, HC, D], FP32R), sb("w2_lo", [P, E, HC, D], FP32R)
        stats = sb("stats", [P, TQ, 6])
        mv = sb("mv", [P, TQ, 2])
        var_eps = sb("var_eps", [P, TQ])
        rstd = sb("rstd", [P, TQ])
        xn = sb("xn", [P, TQ, D])
        base = sb("base", [P, 2, TQ, D])
        xT_hi = sb("xT_hi", [P, 2, TILE], FP32R)
        xT_lo = sb("xT_lo", [P, 2, TILE], FP32R)
        r1 = sb("r1", [P, TILE])
        lg = sb("lg", [P, TQ, E])
        lmax = sb("lmax", [P, TQ])
        lgd = sb("lgd", [P, TQ, E])
        above = sb("above", [P, TQ, E, E])
        level = sb("level", [P, TQ, E, E])
        rank = sb("rank", [P, TQ, E])
        sel4 = sb("sel4", [P, TQ, E])
        seld = sb("seld", [P, TQ, E])
        ssum = sb("ssum", [P, TQ])
        tin = sb("tin", [P, TQ, E])
        th = sb("th", [P, TQ, E])
        gate = sb("gate", [P, TQ, E])
        rest = sb("rest", [P, TQ, E])
        parts = sb("parts", [P, TQ, SPLITS * E], BF16)
        gateT = sb("gateT", [SPLITS * E, TILE], BF16)
        gate_bc = sb("gate_bc", [P, 2, TILE])
        hid = sb("hid", [P, 4, TILE])
        hid_hi = sb("hid_hi", [P, 4, TILE], FP32R)
        hid_lo = sb("hid_lo", [P, 4, TILE], FP32R)
        mix = sb("mix", [P, 2, TILE])
        acc = sb("acc", [P, 2, TILE])

        up_ps = [ps(f"up{i}") for i in range(2)]
        down_ps = [ps(f"down{i}") for i in range(2)]
        gate_ps = ps("gate")
        in_ps = ps("in")
        logit_ps = ps("logit")
        out_ps = ps("out")
        gateT_ps = logit_ps[0:SPLITS * E, 0:TILE // 2].bitcast(BF16)

        x_first, x_rest, rows_in, w_in = sem("x_first"), sem("x_rest"), sem("rows_in"), [sem(f"w_in{e}") for e in range(E)]
        rw_in, rows_t, rows_ready, w_hi, w_lo, zeroed, sel_ready = (
            sem("rw_in"), sem("rows_t"), sem("rows_ready"), sem("w_hi"), sem("w_lo"), sem("zeroed"), sem("sel_ready"))
        later_in = sem("later_in")
        s_stats, s_mv, s_vareps, s_rstd, s_xn, s_xnT, s_xhi, s_xlo = (
            sem("stats"), sem("mv"), sem("vareps"), sem("rstd"), sem("xn"), sem("xnT"), sem("xhi"), sem("xlo"))
        s_r1p, s_r1, s_logit, s_router, s_tanh, s_gateTp, s_gateT = (
            sem("r1p"), sem("r1"), sem("logit"), sem("router"), sem("tanh"), sem("gateTp"), sem("gateT"))
        s_outT, s_xnew, s_stored = sem("outT"), sem("xnew"), sem("stored")
        s_gatep, s_gate, s_down, s_mixed, s_added = sem("gatep"), sem("gate"), sem("down"), sem("mixed"), sem("added")
        s_up, s_silu, s_hi3, s_hi, s_lo, s_used = sem("up"), sem("silu"), sem("hi3"), sem("hi"), sem("lo"), sem("used")

        def xcols(tile, q=None):
            if q is None:
                return bass.ds((tile + 1) * TILE, TILE)
            return bass.ds((tile + 1) * TILE + q * D, D)

        extra = 1 if loads else 0

        block = ctx.enter_context(nc.Block())

        @block.sync
        def _(sp):
            if loads:
                def load_x(t, s):
                    sp.dma_start(k.x[:, (t + 1) * TILE:(t + 2) * TILE].rearrange("p (q d) -> p q d", q=TQ),
                                 x_in[t]).then_inc(s, 16)
                load_x(0, x_first)
                for dst, src in loads["rows"]:
                    sp.dma_start(rows[dst], src).then_inc(rows_in, 16)
                sp.dma_start(k.rb2[:, :], loads["rb2"]).then_inc(rows_in, 16)
                sp.dma_start(rawr[:, :], loads["rw1"]).then_inc(rw_in, 16)
                sp.dma_start(k.rw2[:, :], loads["rw2"]).then_inc(rw_in, 16)
            for e in range(0 if loads else RAW, E):
                if e >= RAW:
                    sp.wait_ge(w_lo, e - RAW + 1 + extra)
                load_expert(nc, sp, k, e, w_in[e])
            if loads:
                for t in range(1, TILES):
                    load_x(t, x_rest)
                sp.wait_ge(w_lo, E + extra)
                for dst, src in loads["later"]:
                    sp.dma_start(dst, src).then_inc(later_in, 16)
                sp.wait_ge(later_in, 16 * len(loads["later"]))
            if out is not None:
                with sp.Fori(0, TILES) as t:
                    sp.wait_ge(s_xnew, t + 3)
                    sp.dma_start(out[bass.ds(t * TILE, TILE), :].rearrange("(q p) d -> p q d", p=P),
                                 k.x[:, bass.ds((t + 1) * TILE, TILE)].rearrange("p (q d) -> p q d", q=TQ)).then_inc(s_stored, 16)
                sp.wait_ge(s_stored, 16 * TILES)

        @block.tensor
        def _(pe):
            def xn_transpose(n):
                pe.wait_ge(s_xn, n)
                for q in range(TQ):
                    last = nc.tensor.transpose(in_ps[:, q * P:(q + 1) * P], xn[:, q, :], k.ident[:, :])
                last.then_inc(s_xnT, 1)

            def router_hidden(n, b):
                pe.wait_ge(s_xlo, n)
                nc.tensor.matmul(in_ps[:, :], k.rw1_hi[:, :], xT_hi[:, b, :], start=True, stop=False)
                nc.tensor.matmul(in_ps[:, :], k.rw1_hi[:, :], xT_lo[:, b, :], start=False, stop=False)
                nc.tensor.matmul(in_ps[:, :], k.rw1_lo[:, :], xT_hi[:, b, :], start=False, stop=True).then_inc(s_r1p, 1)

            def logits(n):
                pe.wait_ge(s_r1, n)
                for q in range(TQ):
                    last = nc.tensor.matmul(logit_ps[:, q * E:(q + 1) * E], r1[:, q * P:(q + 1) * P], k.rw2[:, :],
                                            start=True, stop=True)
                last.then_inc(s_logit, 1)

            def gate_transpose(router_done):
                pe.wait_ge(s_router, router_done)
                for q in range(TQ):
                    last = nc.tensor.transpose(gateT_ps[:, q * P:(q + 1) * P], parts[:, q, :], k.ident_bf[:, :])
                last.then_inc(s_gateTp, 1)

            def gate_broadcast(e):
                nc.tensor.matmul(gate_ps[:, :], k.sel[:, e, :], gateT[:, :], start=True, stop=True).then_inc(s_gatep, 1)

            def up(j, b):
                e, c = (j % CH) // HC, j % HC
                u = up_ps[j % 2]
                w = slice(c * P, (c + 1) * P)
                nc.tensor.matmul(u[:, :], w1_hi[:, e, w], xT_hi[:, b, :], start=True, stop=False)
                nc.tensor.matmul(u[:, :], w1_hi[:, e, w], xT_lo[:, b, :], start=False, stop=False)
                nc.tensor.matmul(u[:, :], w1_lo[:, e, w], xT_hi[:, b, :], start=False, stop=True).then_inc(s_up, 1)

            def down(j):
                e, c = j // HC, j % HC
                o = down_ps[e % 2]
                nc.tensor.matmul(o[:, :], w2_hi[:, e, c, :], hid_hi[:, c, :], start=(c == 0), stop=False)
                nc.tensor.matmul(o[:, :], w2_hi[:, e, c, :], hid_lo[:, c, :], start=False, stop=False)
                last = nc.tensor.matmul(o[:, :], w2_lo[:, e, c, :], hid_hi[:, c, :], start=False, stop=(c == HC - 1))
                last.then_inc(s_used, 1)

            pe.sem_inc(s_used, 4)
            if loads:
                pe.wait_ge(zeroed, k.n_zeroed)
                pe.wait_ge(rows_in, 16 * (len(loads["rows"]) + 1))
                nc.tensor.transpose(out_ps[:, 0:ROWS], rows[:, :], k.ident[0:ROWS, 0:ROWS]).then_inc(rows_t, 1)
                pe.wait_ge(sel_ready, k.n_sel)
                pe.wait_ge(rows_ready, 1)
            xn_transpose(1)
            if loads:
                pe.wait_ge(w_lo, 1)
            router_hidden(1, 0)
            if loads:
                pe.wait_ge(rw_in, 32)
            logits(1)
            gate_transpose(RS)
            pe.wait_ge(s_gateT, 1)
            gate_broadcast(0)
            pe.wait_ge(w_lo, 1 + extra)
            for j in range(AHEAD):
                if j >= 2:
                    pe.wait_ge(s_silu, j - 1)
                up(j, 0)

            with pe.Fori(0, TILES // UNROLL) as it:
                chunks, tiles, experts = pe.snap(it * (2 * CH)), pe.snap(it * 2), pe.snap(it * (2 * E))
                routed, added = pe.snap(it * (2 * RS)), pe.snap(it * (2 * (E - 1)))
                for b in range(UNROLL):
                    for j in range(CH):
                        e, c = j // HC, j % HC
                        g = b * CH + j
                        if c == 0:
                            pe.wait_ge(s_gate, experts + (b * E + e + 1))
                            if e == E - 1:
                                pe.wait_ge(s_gateT, tiles + (b + 2))
                            gate_broadcast((e + 1) % E)
                        if j == 3:
                            pe.wait_ge(s_added, added + (b * (E - 1) + 1))
                            pe.wait_ge(s_xnew, tiles + (b + 1))
                            for q in range(TQ):
                                last = nc.tensor.transpose(out_ps[:, q * P:(q + 1) * P], acc[:, 1 - b, q * P:(q + 1) * P],
                                                           k.ident[:, :])
                            last.then_inc(s_outT, 1)
                        if j == 7:
                            xn_transpose(tiles + (b + 2))
                        if j == 10:
                            router_hidden(tiles + (b + 2), 1 - b)
                        if j == 13:
                            logits(tiles + (b + 2))
                        if j == 25:
                            gate_transpose(routed + (b + 2) * RS)
                        pe.wait_ge(s_lo, chunks + (g + 1))
                        if c == 0:
                            pe.wait_ge(s_mixed, experts + (b * E + e + 1))
                        down(j)
                        pe.wait_ge(s_silu, chunks + (g + AHEAD - 1))
                        if b == 0 and j + AHEAD < CH and (j + AHEAD) % HC == 0:
                            pe.wait_ge(w_lo, (j + AHEAD) // HC + 1 + extra)
                        up(j + AHEAD, b if j + AHEAD < CH else 1 - b)
            pe.wait_ge(s_added, TILES * (E - 1) + 1)
            pe.wait_ge(s_xnew, TILES + 1)
            for q in range(TQ):
                last = nc.tensor.transpose(out_ps[:, q * P:(q + 1) * P], acc[:, 1, q * P:(q + 1) * P], k.ident[:, :])
            last.then_inc(s_outT, 1)

        @block.scalar
        def _(act):
            def x_hi(n, b):
                act.wait_ge(s_xnT, n)
                nc.scalar.activation(xT_hi[:, b, :], in_ps[:, :], ACT.Copy).then_inc(s_xhi, 1)

            def router_silu(n):
                act.wait_ge(s_r1p, n)
                nc.scalar.activation(r1[:, :], in_ps[:, :], ACT.Silu,
                                     bias=k.cols[:, ROW_RB1:ROW_RB1 + 1]).then_inc(s_r1, 1)

            def router_tanh(step12):
                act.wait_ge(s_router, step12)
                nc.scalar.activation(th[:, :, :], tin[:, :, :], ACT.Tanh).then_inc(s_tanh, 1)

            def gate_transposed(n):
                act.wait_ge(s_gateTp, n)
                nc.scalar.activation(gateT[:, :], gateT_ps, ACT.Copy).then_inc(s_gateT, 1)

            def gate_copy(e, n):
                act.wait_ge(s_gatep, n)
                nc.scalar.activation(gate_bc[:, e % 2, :], gate_ps[:, :], ACT.Copy).then_inc(s_gate, 1)

            def silu(j, n):
                e, c = (j % CH) // HC, j % HC
                act.wait_ge(s_up, n)
                col = ROW_BE1 + e * HC + c
                nc.scalar.activation(hid[:, c, :], up_ps[j % 2][:, :], ACT.Silu,
                                     bias=k.cols[:, col:col + 1]).then_inc(s_silu, 1)

            if loads:
                act.wait_ge(rw_in, 32)
                nc.scalar.activation(k.rw1_hi[:, :], rawr[:, :], ACT.Copy).then_inc(w_hi, 1)
            x_hi(1, 0)
            if loads:
                act.wait_ge(rows_ready, 1)
            router_silu(1)
            for e in range(E):
                if loads or e >= RAW:
                    act.wait_ge(w_in[e], 32)
                nc.scalar.activation(w1_hi[:, e, :], k.raw1[:, e % RAW, :], ACT.Copy)
                nc.scalar.activation(w2_hi[:, e, :, :], k.raw2[:, e % RAW, :, :], ACT.Copy).then_inc(w_hi, 1)
            router_tanh(12)
            gate_transposed(1)
            gate_copy(0, 1)
            for j in range(AHEAD):
                silu(j, j + 1)

            with act.Fori(0, TILES // UNROLL) as it:
                chunks, tiles, experts = act.snap(it * (2 * CH)), act.snap(it * 2), act.snap(it * (2 * E))
                routed = act.snap(it * (2 * RS))
                for b in range(UNROLL):
                    for j in range(CH):
                        e, c = j // HC, j % HC
                        g = b * CH + j
                        if c == 0:
                            act.wait_ge(s_silu, chunks + (g + HC))
                            act.wait_ge(s_used, chunks + (g + HC))
                            nc.scalar.activation(hid_hi[:, HC - 1, :], hid[:, HC - 1, :], ACT.Copy).then_inc(s_hi3, 1)
                        act.wait_ge(s_lo, chunks + (g + 1))
                        silu(j + AHEAD, chunks + (g + AHEAD + 1))
                        if c == 0:
                            act.wait_ge(s_mixed, experts + (b * E + e + 2))
                            gate_copy(e + 1, experts + (b * E + e + 2))
                        if j == 8:
                            x_hi(tiles + (b + 2), 1 - b)
                        if j == 11:
                            router_silu(tiles + (b + 2))
                        if j == 20:
                            router_tanh(routed + (b + 1) * RS + 12)
                        if j == 25:
                            gate_transposed(tiles + (b + 2))

        @block.gpsimd
        def _(pool):
            if loads:
                k.make_constants(nc, pool, zeroed, sel_ready)
                pool.wait_ge(zeroed, k.n_zeroed)
            nc.gpsimd.memset(acc[:, 1, :], 0.0).then_inc(s_added, 1)

            def inverse_std(n):
                pool.wait_ge(s_mv, n)
                nc.gpsimd.tensor_tensor(var_eps[:, :], mv[:, :, 1], k.eps[:, 0:TQ], ALU.add).then_inc(s_vareps, 1)
                pool.wait_ge(s_vareps, n)
                nc.gpsimd.tensor_tensor(rstd[:, :], var_eps[:, :], k.minus_half[:, 0:TQ], ALU.pow).then_inc(s_rstd, 1)

            inverse_std(1)
            with pool.Fori(0, TILES // UNROLL) as it:
                tiles, experts, added = pool.snap(it * 2), pool.snap(it * (2 * E)), pool.snap(it * (2 * (E - 1)))
                for b in range(UNROLL):
                    inverse_std(tiles + (b + 2))
                    for e in range(1, E):
                        pool.wait_ge(s_mixed, experts + (b * E + e + 3))
                        pool.wait_ge(s_added, added + (b * (E - 1) + e))
                        nc.gpsimd.tensor_tensor(acc[:, b, :], acc[:, b, :], mix[:, e % 2, :], ALU.add).then_inc(s_added, 1)

        @block.vector
        def _(dve):
            v = nc.vector

            def stats_of(tile, q):
                return v.bn_stats(stats[:, q, :], k.x[:, xcols(tile, q)])

            def aggregate():
                for q in range(TQ):
                    last = v.bn_aggr(mv[:, q, :], stats[:, q, :])
                last.then_inc(s_mv, 1)

            def normalise(tile, q):
                return v.tensor_scalar(xn[:, q, :], k.x[:, xcols(tile, q)], mv[:, q, 0:1], rstd[:, q:q + 1],
                                       ALU.subtract, ALU.mult)

            def make_base(tile, n, b):
                dve.wait_ge(s_xn, n)
                v.scalar_tensor_tensor(base[:, b, :, :].rearrange("p q d -> p (q d)"), xn[:, :, :].rearrange("p q d -> p (q d)"), 0.5,
                                       k.x[:, xcols(tile)], ALU.mult, ALU.add)

            def x_lo(n, b):
                dve.wait_ge(s_xhi, n)
                v.tensor_tensor(xT_lo[:, b, :], in_ps[:, :], xT_hi[:, b, :].bitcast(FP32), ALU.subtract).then_inc(s_xlo, 1)

            def bc(ap):
                return ap.unsqueeze(2).broadcast_to([P, TQ, E])

            def router(i, n, r):
                if i >= 2 and i not in (5, 10):
                    dve.wait_ge(s_router, r + (i - 1))
                if i == 1:
                    dve.wait_ge(s_logit, n)
                    ins = v.tensor_tensor(lg[:, :, :], logit_ps[:, 0:TQ * E].rearrange("p (q e) -> p q e", q=TQ),
                                          k.rb2[:, :].unsqueeze(1).broadcast_to([P, TQ, E]), ALU.add)
                if i == 2:
                    ins = v.tensor_reduce(lmax[:, :], lg[:, :, :], AXIS_X, ALU.max)
                if i == 3:
                    ins = v.tensor_tensor(lgd[:, :, :], lg[:, :, :], bc(lmax[:, :]), ALU.subtract)
                mine = lgd[:, :, :].unsqueeze(3).broadcast_to([P, TQ, E, E])
                others = lgd[:, :, :].unsqueeze(2).broadcast_to([P, TQ, E, E])
                if i == 4:
                    ins = v.tensor_tensor(above[:, :, :, :], others, mine, ALU.is_gt)
                if i == 5:
                    ins = v.tensor_tensor(level[:, :, :, :], others, mine, ALU.is_equal)
                if i == 6:
                    ins = v.tensor_tensor(level[:, :, :, :], level[:, :, :, :],
                                          k.earlier[:, :, :].unsqueeze(1).broadcast_to([P, TQ, E, E]), ALU.mult)
                if i == 7:
                    ins = v.tensor_tensor(above[:, :, :, :], above[:, :, :, :], level[:, :, :, :], ALU.add)
                if i == 8:
                    ins = v.tensor_reduce(rank[:, :, :], above[:, :, :, :], AXIS_X, ALU.add)
                if i == 9:
                    ins = v.tensor_scalar(sel4[:, :, :], rank[:, :, :], 1.5, 0.25, ALU.is_lt, ALU.mult)
                if i == 10:
                    dve.wait_ge(s_router, r + 9)
                    ins = v.tensor_tensor(seld[:, :, :], sel4[:, :, :], lgd[:, :, :], ALU.mult)
                if i == 11:
                    ins = v.tensor_reduce(ssum[:, :], seld[:, :, :], AXIS_X, ALU.add)
                if i == 12:
                    ins = v.scalar_tensor_tensor(tin[:, :, :], bc(ssum[:, :]), -2.0, lgd[:, :, :], ALU.mult, ALU.add)
                if i == 13:
                    dve.wait_ge(s_tanh, n)
                    ins = v.scalar_tensor_tensor(gate[:, :, :], th[:, :, :], 1.0, sel4[:, :, :], ALU.add, ALU.mult)
                if i == 14:
                    ins = v.tensor_copy(parts[:, :, 0:E], gate[:, :, :])
                if i == 15:
                    ins = v.tensor_tensor(rest[:, :, :], gate[:, :, :], parts[:, :, 0:E], ALU.subtract)
                if i == 16:
                    ins = v.tensor_copy(parts[:, :, E:2 * E], rest[:, :, :])
                if i == 17:
                    ins = v.tensor_tensor(parts[:, :, 2 * E:3 * E], rest[:, :, :], parts[:, :, E:2 * E], ALU.subtract)
                ins.then_inc(s_router, 1)

            def hid_high(c, n):
                dve.wait_ge(s_silu, n)
                dve.wait_ge(s_used, n)
                v.tensor_copy(hid_hi[:, c, :], hid[:, c, :]).then_inc(s_hi, 1)

            def hid_low(c, n3):
                dve.wait_ge(s_hi3 if c == HC - 1 else s_hi, n3)
                v.tensor_tensor(hid_lo[:, c, :], hid[:, c, :], hid_hi[:, c, :].bitcast(FP32), ALU.subtract).then_inc(s_lo, 1)

            def add_out(tile, n, b):
                dve.wait_ge(s_outT, n)
                v.tensor_tensor(k.x[:, xcols(tile)], out_ps[:, :], base[:, b, :, :].rearrange("p q d -> p (q d)"), ALU.add).then_inc(s_xnew, 1)

            dve.sem_inc(s_mixed, 2)
            v.memset(base[:, 1, :, :], 0.0).then_inc(s_xnew, 1)
            if loads:
                dve.wait_ge(x_first, 16)
            for q in range(TQ):
                last = stats_of(0, q)
            last.then_inc(s_stats, 1)
            dve.wait_ge(s_stats, 1)
            aggregate()
            if loads:
                dve.wait_ge(rows_t, 1)
                v.tensor_copy(k.cols[:, :], out_ps[:, 0:ROWS]).then_inc(rows_ready, 1)
                dve.wait_ge(zeroed, k.n_zeroed)
                dve.wait_ge(sel_ready, k.n_sel)
                dve.wait_ge(w_hi, 1)
                v.tensor_tensor(k.rw1_lo[:, :], rawr[:, :], k.rw1_hi[:, :].bitcast(FP32), ALU.subtract).then_inc(w_lo, 1)
            dve.wait_ge(s_rstd, 1)
            for q in range(TQ):
                last = normalise(0, q)
            last.then_inc(s_xn, 1)
            make_base(0, 1, 0)
            x_lo(1, 0)
            for i in range(1, 13):
                router(i, 1, 0)
            for e in range(E):
                dve.wait_ge(w_hi, e + 1 + extra)
                v.tensor_tensor(w1_lo[:, e, :], k.raw1[:, e % RAW, :], w1_hi[:, e, :].bitcast(FP32), ALU.subtract)
                v.tensor_tensor(w2_lo[:, e, :, :], k.raw2[:, e % RAW, :, :], w2_hi[:, e, :, :].bitcast(FP32),
                                ALU.subtract).then_inc(w_lo, 1)
            for i in range(13, RS + 1):
                router(i, 1, 0)
            for c in range(3):
                hid_high(c, c + 1)
                if c < 2:
                    hid_low(c, c + 1)
            if loads:
                dve.wait_ge(x_rest, 16 * (TILES - 1))

            with dve.Fori(0, TILES // UNROLL) as it:
                chunks, tiles, experts = dve.snap(it * (2 * CH)), dve.snap(it * 2), dve.snap(it * (2 * E))
                highs, routed, added = dve.snap(it * (2 * E * 3)), dve.snap(it * (2 * RS)), dve.snap(it * (2 * (E - 1)))
                cols = tiles
                for b in range(UNROLL):
                    nxt = b + 2
                    for j in range(CH):
                        e, c = j // HC, j % HC
                        g = b * CH + j
                        if j == 0:
                            stats_of(cols + (b + 1), 0)
                            stats_of(cols + (b + 1), 1)
                        if j == 3:
                            dve.wait_ge(s_rstd, tiles + nxt)
                            normalise(cols + (b + 1), 0)
                            normalise(cols + (b + 1), 1)
                        if j == 9:
                            x_lo(tiles + nxt, 1 - b)
                        if 14 <= j < 19:
                            router(2 * (j - 14) + 1, tiles + nxt, routed + (b + 1) * RS)
                        if j == 19:
                            router(11, tiles + nxt, routed + (b + 1) * RS)
                        if j == 21:
                            router(13, tiles + nxt, routed + (b + 1) * RS)
                        if j == 22:
                            router(15, tiles + nxt, routed + (b + 1) * RS)
                        if j == 23:
                            router(17, tiles + nxt, routed + (b + 1) * RS)
                        if j == 1:
                            dve.wait_ge(s_stats, tiles + nxt)
                        jh, jl = g + 3, g + 2
                        if jh % HC != HC - 1:
                            dve.wait_ge(s_silu, chunks + (jh + 1))
                            dve.wait_ge(s_used, chunks + (jh + 1))
                            v.tensor_copy(hid_hi[:, jh % HC, :], hid[:, jh % HC, :]).then_inc(s_hi, 1)
                        if jl % HC == HC - 1:
                            hid_low(jl % HC, experts + (jl // HC + 1))
                        else:
                            hid_low(jl % HC, highs + (3 * (jl // HC) + jl % HC + 1))
                        if j == 0:
                            stats_of(cols + (b + 1), 2)
                            stats_of(cols + (b + 1), 3).then_inc(s_stats, 1)
                        if j == 1:
                            aggregate()
                        if j == 3:
                            normalise(cols + (b + 1), 2)
                            normalise(cols + (b + 1), 3).then_inc(s_xn, 1)
                        if j == 4:
                            add_out(cols + (b - 1), tiles + (b + 1), 1 - b)
                        if j == 6:
                            make_base(cols + (b + 1), tiles + nxt, 1 - b)
                        if 14 <= j < 19:
                            router(2 * (j - 14) + 2, tiles + nxt, routed + (b + 1) * RS)
                        if j == 19:
                            router(12, tiles + nxt, routed + (b + 1) * RS)
                        if j == 21:
                            router(14, tiles + nxt, routed + (b + 1) * RS)
                        if j == 22:
                            router(16, tiles + nxt, routed + (b + 1) * RS)
                        if c == HC - 1:
                            dve.wait_ge(s_used, chunks + (g + 1 + 4))
                            dve.wait_ge(s_gate, experts + (b * E + e + 1))
                            if e == 0:
                                to = acc[:, b, :]
                            else:
                                to = mix[:, e % 2, :]
                                prior = b * (E - 1) + max(e - 2, 0) + 1
                                dve.wait_ge(s_added, added + prior)
                            col = ROW_BE2 + e
                            v.scalar_tensor_tensor(to, down_ps[e % 2][:, :], k.cols[:, col:col + 1], gate_bc[:, e % 2, :],
                                                   ALU.add, ALU.mult).then_inc(s_mixed, 1)
            add_out(TILES - 1, TILES + 1, 1)



def attention_phase(nc, k, out=None):
    NB = k.tiles * TILE // BT
    DH = 64
    UNITS = 4
    FILLS = 12
    PROJ = 3 * UNITS
    PAIRS = AH // P
    NRING = 4
    BQ = BT // P
    name = "at"
    with ExitStack() as ctx:
        def sb(n, shape, dt=FP32):
            return ctx.enter_context(nc.sbuf_tensor(f"{name}_{n}", shape, dt))

        def ps(n):
            return ctx.enter_context(nc.psum_tensor(f"{name}_{n}_ps", [P, 512], FP32))

        def sem(n):
            return ctx.enter_context(nc.semaphore(f"{name}_{n}_sem"))

        wq_hi, wk_hi, wv_hi = [sb(f"w{n}_hi", [P, AH], FP32R) for n in "qkv"]
        wq_lo, wk_lo, wv_lo = [sb(f"w{n}_lo", [P, AH], FP32R) for n in "qkv"]
        wf1_hi, wf1_lo = sb("wf1_hi", [P, HID], FP32R), sb("wf1_lo", [P, HID], FP32R)
        mask = sb("mask", [P, 3, P])
        den_sel = sb("den_sel", [P, UNITS, 32])
        head_sel_f = sb("head_sel_f", [P, PAIRS, 2, DH])
        head_sel = sb("head_sel", [P, PAIRS, P], FP32R)
        st = {n: sb(f"stats_{n}", [P, BQ, 6]) for n in "ABC"}
        mv = {n: sb(f"mv_{n}", [P, BQ, 2]) for n in "ABC"}
        ve = {n: sb(f"ve_{n}", [P, BQ]) for n in "ABC"}
        rs = {n: sb(f"rs_{n}", [P, BQ]) for n in "ABC"}
        y = sb("y", [P, NRING, BQ, D])
        z = sb("z", [P, BQ, D])
        hT = sb("hT", [P, BT])
        hT_hi, hT_lo = sb("hT_hi", [P, 2, BT], FP32R), sb("hT_lo", [P, 2, BT], FP32R)
        exps, relus = sb("exps", [P, 2, 2 * BT]), sb("relus", [P, 2, 2 * BT])
        qk = sb("qk", [P, PAIRS, 2, BT])
        vals = sb("vals", [P, 2, BQ, AH])
        sc = sb("sc", [P, 2, 4, 3, P])
        num = sb("num", [P, 2, UNITS, 2 * BT])
        den = sb("den", [P, BT])
        rden = sb("rden", [P, BT])
        rden_hi, rden_lo = sb("rden_hi", [P, BT], FP32R), sb("rden_lo", [P, BT], FP32R)
        attnT = sb("attnT", [P, BT])
        a_nat = sb("a_nat", [P, BQ, D])
        xa = sb("xa", [P, BQ, D])
        an = sb("an", [P, BQ, D])
        h2 = sb("h2", [P, BT])
        h2_hi, h2_lo = sb("h2_hi", [P, BT], FP32R), sb("h2_lo", [P, BT], FP32R)
        gel = sb("gel", [P, HC, BT])
        ffnT = sb("ffnT", [P, BT])

        s_ps = [ps(f"s{i}") for i in range(4)]
        proj_ps, num_ps, den_ps, slot_ps = ps("proj"), ps("num"), ps("den"), ps("slot")

        s_split_hi, s_split_lo, s_const, s_sel, w_next, s_zero = (
            sem("split_hi"), sem("split_lo"), sem("const"), sem("sel"), sem("w_next"), sem("zero"))
        s_stored = sem("stored")
        s_st = {n: sem(f"st{n}") for n in "ABC"}
        s_mv = {n: sem(f"mv{n}") for n in "ABC"}
        s_ve = {n: sem(f"ve{n}") for n in "ABC"}
        s_rs = {n: sem(f"rs{n}") for n in "ABC"}
        s_y, s_z, s_hT, s_hT_hi, s_hT_lo = sem("y"), sem("z"), sem("hT"), sem("hT_hi"), sem("hT_lo")
        s_proj, s_proj_out, s_exp, s_phi = sem("proj"), sem("proj_out"), sem("exp"), sem("phi")
        s_score, s_masked, s_quad, s_num, s_num_out = sem("score"), sem("masked"), sem("quad"), sem("num"), sem("num_out")
        s_den, s_rden, s_rhi, s_rlo = sem("den"), sem("rden"), sem("rhi"), sem("rlo")
        s_slot = sem("slot")
        s_o, s_attnT, s_a, s_xa, s_an, s_h2, s_h2_hi, s_h2_lo, s_gelu, s_ffnT, s_x = (
            sem("o"), sem("attnT"), sem("a"), sem("xa"), sem("an"), sem("h2"), sem("h2_hi"), sem("h2_lo"),
            sem("gelu"), sem("ffnT"), sem("x"))

        def xc(s, q=None):
            if q is None:
                return bass.ds((s + 2) * BT, BT)
            return bass.ds((s + 2) * BT + q * D, D)

        def flat(ap):
            return ap.rearrange("p a b -> p (a b)")

        block = ctx.enter_context(nc.Block())

        @block.sync
        def _(sp):
            sp.wait_ge(s_split_lo, 4)
            for e in range(RAW):
                load_expert(nc, sp, k, e, w_next)
            if out is not None:
                with sp.Fori(0, NB) as s:
                    sp.wait_ge(s_x, s + 3)
                    sp.dma_start(out[bass.ds(s * BT, BT), :].rearrange("(q p) d -> p q d", p=P),
                                 k.x[:, bass.ds((s + 2) * BT, BT)].rearrange("p (q d) -> p q d", q=BQ)).then_inc(s_stored, 16)
                sp.wait_ge(s_stored, 16 * NB)
            sp.wait_ge(w_next, 32 * RAW)

        @block.tensor
        def _(pe):
            mm = nc.tensor.matmul

            def transpose_slot(src):
                for q in range(BQ):
                    last = nc.tensor.transpose(slot_ps[:, q * P:(q + 1) * P], src(q), k.ident[:, :])
                last.then_inc(s_slot, 1)

            def ffn_up(c0):
                for i in range(2):
                    o, w = slot_ps[:, i * BT:(i + 1) * BT], slice((c0 + i) * P, (c0 + i + 1) * P)
                    mm(o, wf1_hi[:, w], h2_hi[:, :], start=True, stop=False)
                    mm(o, wf1_hi[:, w], h2_lo[:, :], start=False, stop=False)
                    last = mm(o, wf1_lo[:, w], h2_hi[:, :], start=False, stop=True)
                last.then_inc(s_slot, 1)

            def ffn_down():
                for c in range(HC):
                    last = mm(slot_ps[:, 0:BT], k.wf2[:, c, :], gel[:, c, :], start=(c == 0), stop=(c == HC - 1))
                last.then_inc(s_slot, 1)

            def broadcast(i):
                for cc in range(2):
                    o, sel = slot_ps[:, cc * BT:(cc + 1) * BT], head_sel[:, 2 * i + cc, :]
                    mm(o, sel, rden_hi[:, :], start=True, stop=False)
                    last = mm(o, sel, rden_lo[:, :], start=False, stop=True)
                last.then_inc(s_slot, 1)

            def output_product(par):
                for c in range(PAIRS):
                    last = mm(slot_ps[:, 0:BT], k.wo[:, c, :], num[:, par, c // 2, (c % 2) * BT:(c % 2 + 1) * BT],
                              start=(c == 0), stop=(c == PAIRS - 1))
                last.then_inc(s_slot, 1)

            def project_qk(c, b, n):
                if n is not None:
                    pe.wait_ge(s_proj_out, n - 1)
                w = slice(c * P, (c + 1) * P)
                for i, (hi, lo) in enumerate(((wq_hi, wq_lo), (wk_hi, wk_lo))):
                    o = proj_ps[:, i * BT:(i + 1) * BT]
                    mm(o, hi[:, w], hT_hi[:, b, :], start=True, stop=False)
                    mm(o, hi[:, w], hT_lo[:, b, :], start=False, stop=False)
                    last = mm(o, lo[:, w], hT_hi[:, b, :], start=False, stop=True)
                last.then_inc(s_proj, 1)

            def project_v(u, b, n):
                pe.wait_ge(s_proj_out, n - 1)
                t, w = slice((u % BQ) * P, (u % BQ + 1) * P), slice((u // BQ) * 512, (u // BQ + 1) * 512)
                mm(proj_ps[:, :], hT_hi[:, b, t], wv_hi[:, w], start=True, stop=False)
                mm(proj_ps[:, :], hT_lo[:, b, t], wv_hi[:, w], start=False, stop=False)
                mm(proj_ps[:, :], hT_hi[:, b, t], wv_lo[:, w], start=False, stop=True).then_inc(s_proj, 1)

            def scores(c):
                for half in range(2):
                    r, o = slice(half * DH, (half + 1) * DH), s_ps[2 * (c % 2) + half]
                    mm(o[:, 0:BT], qk[r, c, 1, 0:P], qk[r, c, 0, :], start=True, stop=True)
                for half in range(2):
                    r, o = slice(half * DH, (half + 1) * DH), s_ps[2 * (c % 2) + half]
                    last = mm(o[:, BT:BT + P], qk[r, c, 1, P:BT], qk[r, c, 0, P:BT], start=True, stop=True)
                last.then_inc(s_score, 1)

            def values(u, b):
                for cc in range(2):
                    o = num_ps[:, cc * BT:(cc + 1) * BT]
                    for half in range(2):
                        h = 4 * u + 2 * cc + half
                        r, s4 = slice(half * DH, (half + 1) * DH), sc[:, u % 2, 2 * cc + half, :, :]
                        mm(o[r, :], vals[:, b % 2, 0, h * DH:(h + 1) * DH], flat(s4[:, 0:2, :]), start=True, stop=False)
                    for half in range(2):
                        h = 4 * u + 2 * cc + half
                        r, s4 = slice(half * DH, (half + 1) * DH), sc[:, u % 2, 2 * cc + half, :, :]
                        last = mm(o[r, P:BT], vals[:, b % 2, 1, h * DH:(h + 1) * DH], s4[:, 2, :], start=False, stop=True)
                last.then_inc(s_num, 1)

            def denominators(u):
                for j in range(4):
                    mm(den_ps[32 * j:32 * j + 32, 0:BT], den_sel[:, u, :], flat(sc[:, u % 2, j, 0:2, :]),
                       start=(u == 0), stop=False)
                for j in range(4):
                    last = mm(den_ps[32 * j:32 * j + 32, P:BT], den_sel[:, u, :], sc[:, u % 2, j, 2, :],
                              start=False, stop=(u == UNITS - 1))
                last.then_inc(s_quad, 1)

            pe.sem_inc(s_quad, 1)
            for i in range(2):
                if i:
                    pe.wait_ge(s_hT, i)
                pe.wait_ge(s_z, i + 1)
                transpose_slot(lambda q: z[:, q, :])
            pe.wait_ge(s_hT_lo, 2)
            pe.wait_ge(s_split_lo, 4)
            for u in range(UNITS):
                for cc in range(2):
                    project_qk(2 * u + cc, 0, 3 * u + cc + 1 if u + cc else None)
                project_v(u, 0, 3 * u + 3)
            for cc in range(2):
                pe.wait_ge(s_phi, cc + 1)
                scores(cc)
            pe.wait_ge(s_const, k.n_attn_const)
            pe.wait_ge(s_zero, 5)

            with pe.Fori(0, NB // NRING) as it:
                ones, twos, fours, eights, twelves = (pe.snap(it * (NRING * m)) for m in (1, 2, 4, 8, 12))
                for b in range(NRING):
                    for u in range(UNITS):
                        proj = twelves + (12 * b + 3 * u + 12)
                        for cc in range(2):
                            pe.wait_ge(s_phi, eights + (8 * b + 2 * (u + 1) + cc + 1))
                            pe.wait_ge(s_masked, eights + (8 * b + 2 * u + cc + 1))
                            scores((2 * (u + 1) + cc) % PAIRS)
                            if u == 0 and cc == 0:
                                pe.wait_ge(s_hT_lo, ones + (b + 2))
                            project_qk(2 * u + cc, (b + 1) % 2, proj + (cc + 1))
                            if (u, cc) == (0, 0):
                                pe.wait_ge(s_gelu, twos + (2 * b + 2))
                                ffn_down()
                            if (u, cc) == (0, 1):
                                pe.wait_ge(s_rlo, ones + (b + 1))
                                pe.wait_ge(s_ffnT, ones + (b + 1))
                                broadcast(0)
                            if (u, cc) == (1, 0):
                                pe.wait_ge(s_x, ones + (b + 1))
                                broadcast(1)
                            if (u, cc) == (1, 1):
                                pe.wait_ge(s_o, fours + (4 * b + 2))
                                broadcast(2)
                            if (u, cc) == (2, 0):
                                pe.wait_ge(s_o, fours + (4 * b + 4))
                                output_product((b + 1) % 2)
                            if (u, cc) == (2, 1):
                                pe.wait_ge(s_attnT, ones + (b + 1))
                                transpose_slot(lambda q: attnT[:, q * P:(q + 1) * P])
                            if (u, cc) == (3, 0):
                                pe.wait_ge(s_an, ones + (b + 1))
                                pe.wait_ge(s_hT, ones + (b + 3))
                                transpose_slot(lambda q: an[:, q, :])
                            if (u, cc) == (3, 1):
                                pe.wait_ge(s_h2_lo, ones + (b + 1))
                                ffn_up(0)
                        project_v(u, (b + 1) % 2, proj + 3)
                        pe.wait_ge(s_masked, eights + (8 * b + 2 * u + 2))
                        pe.wait_ge(s_num_out, fours + (4 * b + u + 4))
                        if u == 0:
                            pe.wait_ge(s_proj_out, twelves + (12 * b + 12))
                        values(u, b)
                        if u == 0:
                            pe.wait_ge(s_o, fours + (4 * b + 1))
                            transpose_slot(lambda q: ffnT[:, q * P:(q + 1) * P])
                        if u == 1:
                            pe.wait_ge(s_o, fours + (4 * b + 3))
                            broadcast(3)
                        if u == 2:
                            pe.wait_ge(s_z, ones + (b + 3))
                            pe.wait_ge(s_a, ones + (b + 1))
                            transpose_slot(lambda q: z[:, q, :])
                        if u == 3:
                            pe.wait_ge(s_gelu, twos + (2 * b + 3))
                            ffn_up(2)
                        if u == 0:
                            pe.wait_ge(s_den, ones + (b + 1))
                        denominators(u)
            pe.wait_ge(s_gelu, 2 * NB + 2)
            ffn_down()
            pe.wait_ge(s_ffnT, NB + 1)
            transpose_slot(lambda q: ffnT[:, q * P:(q + 1) * P])
            pe.wait_ge(s_rlo, NB + 1)
            pe.wait_ge(s_x, NB + 1)
            for i in range(UNITS):
                if i:
                    pe.wait_ge(s_o, 4 * NB + i)
                broadcast(i)
            pe.wait_ge(s_o, 4 * NB + 4)
            output_product((NB + 1) % 2)
            pe.wait_ge(s_attnT, NB + 1)
            transpose_slot(lambda q: attnT[:, q * P:(q + 1) * P])
            pe.wait_ge(s_an, NB + 1)
            transpose_slot(lambda q: an[:, q, :])
            pe.wait_ge(s_h2_lo, NB + 1)
            ffn_up(0)
            pe.wait_ge(s_gelu, 2 * NB + 3)
            ffn_up(2)
            pe.wait_ge(s_gelu, 2 * NB + 4)
            ffn_down()
            pe.wait_ge(s_ffnT, NB + 2)
            transpose_slot(lambda q: ffnT[:, q * P:(q + 1) * P])

        @block.scalar
        def _(act):
            A = nc.scalar.activation

            def phi_parts(c, n, n_phi):
                act.wait_ge(s_proj, n)
                if n_phi is not None:
                    act.wait_ge(s_phi, n_phi)
                A(exps[:, c % 2, :], proj_ps[:, :], ACT.Exp).then_inc(s_exp, 1)
                A(relus[:, c % 2, :], proj_ps[:, :], ACT.Relu).then_inc(s_proj_out, 1)

            def copy_v(u, b, n):
                act.wait_ge(s_proj, n)
                A(vals[:, b % 2, u % BQ, (u // BQ) * 512:(u // BQ + 1) * 512], proj_ps[:, :], ACT.Copy).then_inc(s_proj_out, 1)

            def affine(dst, g_col, n, s):
                act.wait_ge(s_slot, n)
                A(dst, slot_ps[:, 0:BT], ACT.Identity, bias=k.cols[:, g_col + 1:g_col + 2],
                  scale=k.cols[:, g_col:g_col + 1]).then_inc(s, 1)

            def gelu(c, n):
                act.wait_ge(s_slot, n)
                A(flat(gel[:, c:c + 2, :]), slot_ps[:, :], ACT.Gelu).then_inc(s_gelu, 1)

            act.sem_inc(s_num_out, 4)
            act.sem_inc(s_gelu, 2)
            for raw, hi in zip(k.raw_qkv + [k.raw_f1], (wq_hi, wk_hi, wv_hi, wf1_hi)):
                A(hi[:, :], raw, ACT.Copy).then_inc(s_split_hi, 1)
            for i in range(2):
                if i:
                    act.wait_ge(s_hT_lo, i)
                affine(hT[:, :], ROW_G1, i + 1, s_hT)
            for u in range(UNITS):
                for cc in range(2):
                    c = 2 * u + cc
                    phi_parts(c, 3 * u + cc + 1, c - 1 if c >= 2 else None)
                copy_v(u, 0, 3 * u + 3)
            act.wait_ge(s_zero, 5)

            with act.Fori(0, NB // NRING) as it:
                ones, fours, eights, twelves = (act.snap(it * (NRING * m)) for m in (1, 4, 8, 12))
                for b in range(NRING):
                    for u in range(UNITS):
                        fill = twelves + (12 * b + 3 * u + 2)
                        proj = twelves + (12 * b + 3 * u + 12)
                        for cc in range(2):
                            c = 2 * u + cc
                            phi_parts(c, proj + (cc + 1), eights + (8 * b + c + 7))
                            slot = 3 * u + cc
                            if slot == 0:
                                act.wait_ge(s_slot, fill + 1)
                                A(ffnT[:, :], slot_ps[:, 0:BT], ACT.Copy).then_inc(s_ffnT, 1)
                            if slot == 6:
                                act.wait_ge(s_slot, fill + 1)
                                A(attnT[:, :], slot_ps[:, 0:BT], ACT.Copy).then_inc(s_attnT, 1)
                            if slot == 9:
                                affine(h2[:, :], ROW_G2, fill + 1, s_h2)
                            if slot == 10:
                                gelu(0, fill + 2)
                        copy_v(u, b + 1, proj + 3)
                        act.wait_ge(s_num, fours + (4 * b + u + 1))
                        A(num[:, b % 2, u, :], num_ps[:, :], ACT.Copy).then_inc(s_num_out, 1)
                        if u == 2:
                            affine(hT[:, :], ROW_G1, fill + 3, s_hT)
                        if u == 3:
                            gelu(2, fill + 3)
            n = 2 + FILLS * NB
            act.wait_ge(s_slot, n + 1)
            A(ffnT[:, :], slot_ps[:, 0:BT], ACT.Copy).then_inc(s_ffnT, 1)
            act.wait_ge(s_slot, n + 7)
            A(attnT[:, :], slot_ps[:, 0:BT], ACT.Copy).then_inc(s_attnT, 1)
            affine(h2[:, :], ROW_G2, n + 9, s_h2)
            gelu(0, n + 10)
            gelu(2, n + 11)
            act.wait_ge(s_slot, n + 12)
            A(ffnT[:, :], slot_ps[:, 0:BT], ACT.Copy).then_inc(s_ffnT, 1)

        @block.gpsimd
        def _(pool):
            g = nc.gpsimd

            def inverse_std(ln, n):
                pool.wait_ge(s_mv[ln], n)
                g.tensor_tensor(ve[ln][:, :], mv[ln][:, :, 1], k.eps[:, 0:BQ], ALU.add).then_inc(s_ve[ln], 1)
                pool.wait_ge(s_ve[ln], n)
                g.tensor_tensor(rs[ln][:, :], ve[ln][:, :], k.minus_half[:, 0:BQ], ALU.pow).then_inc(s_rs[ln], 1)

            for i in range(2):
                inverse_std("A", i + 1)
                inverse_std("B", i + 1)
            g.memset(mask[:, :, :], 1.0).then_inc(s_const, 1)
            g.memset(den_sel[:, :, :], 0.0).then_inc(s_const, 1)
            g.memset(head_sel_f[:, :, :, :], 0.0).then_inc(s_const, 1)
            pool.wait_ge(s_const, 3)
            for blk in (0, 2):
                g.affine_select(out=mask[:, blk, :], in_=mask[:, blk, :], compare_op=ALU.is_ge, fill=0.0, base=0,
                                pattern=[[1, P]], channel_multiplier=-1).then_inc(s_const, 1)
            g.affine_select(out=den_sel[:, :, :], in_=den_sel[:, :, :], compare_op=ALU.not_equal, fill=1.0, base=0,
                            pattern=[[1, UNITS], [-1, 32]], channel_multiplier=0).then_inc(s_const, 1)
            for cc in range(2):
                if cc:
                    pool.wait_ge(s_const, 6 + cc)
                part = head_sel_f[:, cc::2, :, :]
                g.affine_select(out=part, in_=part, compare_op=ALU.not_equal, fill=1.0, base=-64 * cc,
                                pattern=[[-1, UNITS], [-32, 2], [0, DH]], channel_multiplier=1).then_inc(s_const, 1)

            with pool.Fori(0, NB // NRING) as it:
                ones = pool.snap(it * NRING)
                for b in range(NRING):
                    inverse_std("A", ones + (b + 3))
                    inverse_std("B", ones + (b + 3))
                    inverse_std("C", ones + (b + 1))
            inverse_std("C", NB + 1)

        @block.vector
        def _(dve):
            v = nc.vector
            tt, ts, stt = v.tensor_tensor, v.tensor_scalar, v.scalar_tensor_tensor

            def stats(ln, src):
                for q in range(BQ):
                    last = v.bn_stats(st[ln][:, q, :], src(q))
                last.then_inc(s_st[ln], 1)

            def aggregate(ln):
                for q in range(BQ):
                    last = v.bn_aggr(mv[ln][:, q, :], st[ln][:, q, :])
                last.then_inc(s_mv[ln], 1)

            def normalise(ln, n, dst, src, s):
                dve.wait_ge(s_rs[ln], n)
                for q in range(BQ):
                    last = ts(dst(q), src(q), mv[ln][:, q, 0:1], rs[ln][:, q:q + 1], ALU.subtract, ALU.mult)
                last.then_inc(s, 1)

            def split_hT(n, b):
                dve.wait_ge(s_hT, n)
                v.tensor_copy(hT_hi[:, b, :], hT[:, :]).then_inc(s_hT_hi, 1)
                dve.wait_ge(s_hT_hi, n)
                tt(hT_lo[:, b, :], hT[:, :], hT_hi[:, b, :].bitcast(FP32), ALU.subtract).then_inc(s_hT_lo, 1)

            def phi(c, n_out):
                dve.wait_ge(s_proj_out, n_out)
                stt(qk[:, c, :, :].rearrange("p a b -> p (a b)"), exps[:, c % 2, :], 1.0, relus[:, c % 2, :],
                    ALU.min, ALU.add).then_inc(s_phi, 1)

            def mask_scores(cc, par, n):
                dve.wait_ge(s_score, n)
                for half in range(2):
                    last = tt(flat(sc[:, par, 2 * cc + half, :, :]), s_ps[2 * cc + half][:, 0:3 * P], flat(mask[:, :, :]), ALU.mult)
                last.then_inc(s_masked, 1)

            def weigh(i, n, par, n_num):
                dve.wait_ge(s_slot, n)
                dve.wait_ge(s_num_out, n_num + (i + 1))
                tt(num[:, par, i, :], num[:, par, i, :], slot_ps[:, :], ALU.mult).then_inc(s_o, 1)

            v.memset(den_ps[:, 0:BT], 0.0).then_inc(s_zero, 1)
            v.memset(num[:, 1, :, :], 0.0).then_inc(s_zero, 1)
            v.memset(y[:, NRING - 1, :, :], 0.0).then_inc(s_zero, 1)
            v.memset(xa[:, :, :], 0.0).then_inc(s_xa, 1)
            v.memset(gel[:, :, :], 0.0).then_inc(s_zero, 1)
            for i in range(2):
                stats("A", lambda q: k.x[:, xc(i, q)])
                dve.wait_ge(s_st["A"], i + 1)
                aggregate("A")
                normalise("A", i + 1, lambda q: y[:, i, q, :], lambda q: k.x[:, xc(i, q)], s_y)
                dve.wait_ge(s_y, i + 1)
                stats("B", lambda q: y[:, i, q, :])
                dve.wait_ge(s_st["B"], i + 1)
                aggregate("B")
                normalise("B", i + 1, lambda q: z[:, q, :], lambda q: y[:, i, q, :], s_z)
                split_hT(i + 1, i)
            for i, (raw, hi, lo) in enumerate(zip(k.raw_qkv + [k.raw_f1], (wq_hi, wk_hi, wv_hi, wf1_hi),
                                                  (wq_lo, wk_lo, wv_lo, wf1_lo))):
                dve.wait_ge(s_split_hi, i + 1)
                tt(lo[:, :], raw, hi[:, :].bitcast(FP32), ALU.subtract).then_inc(s_split_lo, 1)
            dve.wait_ge(s_const, k.n_attn_const)
            v.tensor_copy(head_sel[:, :, :], head_sel_f[:, :, :, :].rearrange("p c h d -> p c (h d)")).then_inc(s_zero, 1)
            for c in range(PAIRS):
                phi(c, 3 * (c // 2) + c % 2 + 1)
            for cc in range(2):
                mask_scores(cc, 0, cc + 1)
            dve.wait_ge(s_zero, 5)

            with dve.Fori(0, NB // NRING) as it:
                ones, fours, eights, twelves = (dve.snap(it * (NRING * m)) for m in (1, 4, 8, 12))
                for b in range(NRING):
                    s = ones + b
                    for u in range(UNITS):
                        fill = twelves + (12 * b + 3 * u + 2)
                        proj = twelves + (12 * b + 3 * u + 12)
                        if u == 0:
                            dve.wait_ge(s_quad, fours + (4 * b + 1))
                            ts(den[:, :], den_ps[:, 0:BT], EPS_DEN, None, ALU.max).then_inc(s_den, 1)
                        dve.wait_ge(s_quad, fours + (4 * b + u + 1))
                        mask_scores(0, (u + 1) % 2, eights + (8 * b + 2 * u + 3))
                        if u == 0:
                            dve.wait_ge(s_den, ones + (b + 1))
                            v.reciprocal(rden[:, :], den[:, :]).then_inc(s_rden, 1)
                        if u == 3:
                            normalise("C", ones + (b + 1), lambda q: an[:, q, :], lambda q: a_nat[:, q, :], s_an)
                        phi(2 * u, proj + 1)
                        if u == 0:
                            dve.wait_ge(s_rden, ones + (b + 1))
                            v.tensor_copy(rden_hi[:, :], rden[:, :]).then_inc(s_rhi, 1)
                        if u == 1:
                            weigh(1, fill + 1, (b + 1) % 2, fours + 4 * b)
                            normalise("A", ones + (b + 3), lambda q: y[:, (b + 2) % NRING, q, :], lambda q: k.x[:, xc(s + 2, q)], s_y)
                        if u == 2:
                            normalise("B", ones + (b + 3), lambda q: z[:, q, :], lambda q: y[:, (b + 2) % NRING, q, :], s_z)
                        mask_scores(1, (u + 1) % 2, eights + (8 * b + 2 * u + 4))
                        if u == 0:
                            dve.wait_ge(s_rhi, ones + (b + 1))
                            tt(rden_lo[:, :], rden[:, :], rden_hi[:, :].bitcast(FP32), ALU.subtract).then_inc(s_rlo, 1)
                            stats("A", lambda q: k.x[:, xc(s + 2, q)])
                        if u == 3:
                            dve.wait_ge(s_h2, ones + (b + 1))
                            v.tensor_copy(h2_hi[:, :], h2[:, :]).then_inc(s_h2_hi, 1)
                            dve.wait_ge(s_h2_hi, ones + (b + 1))
                            tt(h2_lo[:, :], h2[:, :], h2_hi[:, :].bitcast(FP32), ALU.subtract).then_inc(s_h2_lo, 1)
                        if u == 0:
                            dve.wait_ge(s_st["A"], ones + (b + 3))
                        phi(2 * u + 1, proj + 2)
                        if u == 0:
                            aggregate("A")
                            weigh(0, fill + 2, (b + 1) % 2, fours + 4 * b)
                            dve.wait_ge(s_slot, fill + 3)
                            dve.wait_ge(s_xa, ones + (b + 1))
                            tt(k.x[:, xc(s - 2)], slot_ps[:, 0:BT], flat(xa[:, :, :]), ALU.add).then_inc(s_x, 1)
                        if u == 1:
                            weigh(2, fill + 2, (b + 1) % 2, fours + 4 * b)
                            dve.wait_ge(s_y, ones + (b + 3))
                            stats("B", lambda q: y[:, (b + 2) % NRING, q, :])
                            dve.wait_ge(s_st["B"], ones + (b + 3))
                            weigh(3, fill + 3, (b + 1) % 2, fours + 4 * b)
                            aggregate("B")
                        if u == 2:
                            dve.wait_ge(s_slot, fill + 2)
                            tt(flat(a_nat[:, :, :]), slot_ps[:, 0:BT], flat(y[:, (b + 3) % NRING, :, :]), ALU.add).then_inc(s_a, 1)
                            dve.wait_ge(s_a, ones + (b + 1))
                            stats("C", lambda q: a_nat[:, q, :])
                            dve.wait_ge(s_st["C"], ones + (b + 1))
                            tt(flat(xa[:, :, :]), flat(a_nat[:, :, :]), k.x[:, xc(s - 1)], ALU.add).then_inc(s_xa, 1)
                            aggregate("C")
                            split_hT(ones + (b + 3), b % 2)
            n = 2 + FILLS * NB
            dve.wait_ge(s_quad, 4 * NB + 1)
            ts(den[:, :], den_ps[:, 0:BT], EPS_DEN, None, ALU.max).then_inc(s_den, 1)
            dve.wait_ge(s_den, NB + 1)
            v.reciprocal(rden[:, :], den[:, :]).then_inc(s_rden, 1)
            dve.wait_ge(s_rden, NB + 1)
            v.tensor_copy(rden_hi[:, :], rden[:, :]).then_inc(s_rhi, 1)
            dve.wait_ge(s_rhi, NB + 1)
            tt(rden_lo[:, :], rden[:, :], rden_hi[:, :].bitcast(FP32), ALU.subtract).then_inc(s_rlo, 1)
            dve.wait_ge(s_slot, n + 2)
            dve.wait_ge(s_xa, NB + 1)
            tt(k.x[:, xc(NB - 2)], slot_ps[:, 0:BT], flat(xa[:, :, :]), ALU.add).then_inc(s_x, 1)
            for i in range(UNITS):
                weigh(i, n + 3 + i, (NB + 1) % 2, 4 * NB)
            dve.wait_ge(s_slot, n + 8)
            tt(flat(a_nat[:, :, :]), slot_ps[:, 0:BT], flat(y[:, (NB - 1) % NRING, :, :]), ALU.add).then_inc(s_a, 1)
            dve.wait_ge(s_a, NB + 1)
            stats("C", lambda q: a_nat[:, q, :])
            dve.wait_ge(s_st["C"], NB + 1)
            aggregate("C")
            normalise("C", NB + 1, lambda q: an[:, q, :], lambda q: a_nat[:, q, :], s_an)
            tt(flat(xa[:, :, :]), flat(a_nat[:, :, :]), k.x[:, xc(NB - 1)], ALU.add).then_inc(s_xa, 1)
            dve.wait_ge(s_h2, NB + 1)
            v.tensor_copy(h2_hi[:, :], h2[:, :]).then_inc(s_h2_hi, 1)
            dve.wait_ge(s_h2_hi, NB + 1)
            tt(h2_lo[:, :], h2[:, :], h2_hi[:, :].bitcast(FP32), ALU.subtract).then_inc(s_h2_lo, 1)
            dve.wait_ge(s_slot, n + 13)
            dve.wait_ge(s_xa, NB + 2)
            tt(k.x[:, xc(NB - 1)], slot_ps[:, 0:BT], flat(xa[:, :, :]), ALU.add).then_inc(s_x, 1)


def macaron_kernel(nc, x, ln1_g, ln1_b, wq, wk, wv, wo, ln2_g, ln2_b, wf1, wf2,
                   rw1, rb1, rw2, rb2, we1, be1, we2, be2, out, layers=(1, 2, 3)):
    x_rows, out_rows = x.rearrange("b t d -> (b t) d"), out.rearrange("b t d -> (b t) d")
    ctx = ExitStack()
    with ctx:
        def sb(n, shape, dt=FP32):
            return ctx.enter_context(nc.sbuf_tensor(n, shape, dt))

        k = Kept()
        k.tiles = x_rows.shape[0] // TILE
        k.x = sb("x", [P, (k.tiles + 2) * TILE])
        k.raw1, k.raw2 = sb("raw1", [P, RAW, HID]), sb("raw2", [P, RAW, HC, D])
        k.rw1_hi, k.rw1_lo = sb("rw1_hi", [P, D], FP32R), sb("rw1_lo", [P, D], FP32R)
        k.rw2, k.rb2 = sb("rw2", [P, E]), sb("rb2", [P, E])
        k.cols = sb("cols", [P, ROWS])
        k.ident, k.ident_bf = sb("ident", [P, P]), sb("ident_bf", [P, P], BF16)
        k.sel = sb("sel", [SPLITS * E, E, P], BF16)
        k.earlier = sb("earlier", [P, E, E])
        k.minus_half, k.eps = sb("minus_half", [P, TQ]), sb("eps", [P, TQ])
        k.wo, k.wf2 = sb("wo", [P, AH // P, D]), sb("wf2", [P, HC, D])
        k.raw_qkv = [k.raw1[:, 0:2, :].rearrange("p a n -> p (a n)"), k.raw1[:, 2:4, :].rearrange("p a n -> p (a n)"),
                     k.raw2[:, 0:2, :, :].rearrange("p a c n -> p (a c n)")]
        k.raw_f1 = k.raw2[:, 2, :, :].rearrange("p c n -> p (c n)")

        k.n_zeroed, k.n_sel, k.n_attn_const = 9, SPLITS, 8

        def make_constants(nc, pool, zeroed, sel_ready):
            g = nc.gpsimd
            g.memset(k.ident[:, :], 0.0).then_inc(zeroed, 1)
            g.memset(k.minus_half[:, :], -0.5).then_inc(zeroed, 1)
            g.memset(k.eps[:, :], EPS_LN).then_inc(zeroed, 1)
            g.memset(k.ident_bf[:, :], 0.0).then_inc(zeroed, 1)
            g.memset(k.sel[:, :, :], 0.0).then_inc(zeroed, 1)
            g.memset(k.earlier[:, :, :], 1.0).then_inc(zeroed, 1)
            pool.wait_ge(zeroed, 6)
            for m in (k.ident, k.ident_bf):
                g.affine_select(out=m[:, :], in_=m[:, :], compare_op=ALU.not_equal, fill=1.0, base=0,
                                pattern=[[-1, P]], channel_multiplier=1).then_inc(zeroed, 1)
            g.affine_select(out=k.earlier[:, :, :], in_=k.earlier[:, :, :], compare_op=ALU.is_gt, fill=0.0, base=0,
                            pattern=[[1, E], [-1, E]], channel_multiplier=0).then_inc(zeroed, 1)
            for part in range(SPLITS):
                if part:
                    pool.wait_ge(sel_ready, part)
                g.affine_select(out=k.sel[:, :, :], in_=k.sel[:, :, :], compare_op=ALU.not_equal, fill=1.0,
                                base=-E * part, pattern=[[-1, E], [0, P]], channel_multiplier=1).then_inc(sel_ready, 1)
            g.memset(k.x[:, 0:TILE], 0.0)
            g.memset(k.x[:, (k.tiles + 1) * TILE:(k.tiles + 2) * TILE], 0.0)

        k.make_constants = make_constants
        k.we1, k.we2 = we1, we2

        tile_in = [x_rows[t * TILE:(t + 1) * TILE, :].rearrange("(q p) d -> p q d", p=P) for t in range(k.tiles)]
        row = lambda a: a.rearrange("(a n) -> a n", a=1)
        loads = {
            "rows": [(slice(ROW_BE1, ROW_BE1 + E * HC), be1.rearrange("e (c p) -> (e c) p", p=P)),
                     (slice(ROW_BE2, ROW_BE2 + E), be2), (slice(ROW_RB1, ROW_RB1 + 1), row(rb1)),
                     (slice(ROW_G1, ROW_G1 + 1), row(ln1_g)), (slice(ROW_B1, ROW_B1 + 1), row(ln1_b)),
                     (slice(ROW_G2, ROW_G2 + 1), row(ln2_g)), (slice(ROW_B2, ROW_B2 + 1), row(ln2_b))],
            "rb2": row(rb2).broadcast_to([P, E]),
            "rw1": rw1, "rw2": rw2,
            "later": [(k.raw_qkv[0], wq), (k.raw_qkv[1], wk), (k.raw_qkv[2], wv), (k.raw_f1, wf1),
                      (k.wo[:, :, :], wo.rearrange("(c p) d -> p c d", p=P)), (k.wf2[:, :, :], wf2.rearrange("(c p) d -> p c d", p=P))],
        }
        ffn_phase(nc, k, "f1", x_in=tile_in, loads=loads, out=out_rows if layers == (1,) else None)
        if 2 in layers:
            attention_phase(nc, k, out=out_rows if layers == (1, 2) else None)
        if 3 in layers:
            ffn_phase(nc, k, "f2", out=out_rows)


_INS = ["L0_attn_x", "L0_attn_ln1_g", "L0_attn_ln1_b", "L0_attn_Wq", "L0_attn_Wk", "L0_attn_Wv", "L0_attn_Wo",
        "L0_attn_ln2_g", "L0_attn_ln2_b", "L0_attn_Wf1", "L0_attn_Wf2", "L0_ffn_rw1", "L0_ffn_rb1", "L0_ffn_rw2",
        "L0_ffn_rb2", "L0_ffn_we1", "L0_ffn_be1", "L0_ffn_we2", "L0_ffn_be2"]


def kernel(**inputs):
    import numpy as _np
    import concourse.bacc as _bacc
    from concourse.bass_utils import run_bass_kernel_spmd as _run

    nc = _bacc.Bacc("TRN2", target_bir_lowering=False, num_devices=1)
    arrays, args = {}, []
    for name in _INS:
        a = _np.ascontiguousarray(inputs[name])
        arrays[f"in_{name}"] = a
        args.append(nc.dram_tensor(f"in_{name}", a.shape, mybir.dt.from_np(a.dtype), kind="ExternalInput").ap())
    x = inputs["L0_attn_x"]
    args.append(nc.dram_tensor("out_x", x.shape, FP32, kind="ExternalOutput").ap())
    macaron_kernel(nc, *args)
    r = _run(nc, [arrays], core_ids=[0])
    return r.results[0]["out_x"]
```

```python
from contextlib import ExitStack

import concourse.bass as bass
from concourse import mybir

FP32 = mybir.dt.float32
FP32R = mybir.dt.float32r
BF16 = mybir.dt.bfloat16
ALU = mybir.AluOpType
ACT = mybir.ActivationFunctionType
AXIS_X = mybir.AxisListType.X

P = 128
D = 128
E = 8
HID = 512
HC = HID // P
TILE = 512
TQ = TILE // P
EPS_LN = 1e-5
EPS_DEN = 1e-6
UNROLL = 2
ROUTER_BEFORE = {15: 1, 16: 3, 17: 4, 19: 6, 21: 8, 22: 10, 23: 11, 25: 13, 26: 15, 27: 16}
ROUTER_AFTER = {15: 2, 17: 5, 19: 7, 21: 9, 23: 12, 25: 14, 27: 17}
AHEAD = 4
RS = 17
RAW = 4
EARLY = 3
SPLITS = 3

BT = 256
AH = 1024

ROW_BE1, ROW_BE2, ROW_RB1, ROW_G1, ROW_B1, ROW_G2, ROW_B2, ROWS = 0, 32, 40, 41, 42, 43, 44, 45


def load_expert(nc, sp, k, e, s):
    sp.dma_start(k.raw1[:, e % RAW, :], k.we1[e]).then_inc(s, 16)
    sp.dma_start(k.raw2[:, e % RAW, :, :], k.we2[e].rearrange("(c p) d -> p c d", p=P)).then_inc(s, 16)


class Kept:
    pass


def ffn_phase(nc, k, name, x_in=None, loads=None, out=None):
    TILES = k.tiles
    CH = E * HC
    with ExitStack() as ctx:
        def sb(n, shape, dt=FP32):
            return ctx.enter_context(nc.sbuf_tensor(f"{name}_{n}", shape, dt))

        def ps(n):
            return ctx.enter_context(nc.psum_tensor(f"{name}_{n}_ps", [P, 512], FP32))

        def sem(n):
            return ctx.enter_context(nc.semaphore(f"{name}_{n}_sem"))

        if loads:
            rawr = sb("rawr", [P, D])
            rows = sb("rows", [ROWS, P])
        w1_hi, w1_lo = sb("w1_hi", [P, E, HID], FP32R), sb("w1_lo", [P, E, HID], FP32R)
        w2_hi, w2_lo = sb("w2_hi", [P, E, HC, D], FP32R), sb("w2_lo", [P, E, HC, D], FP32R)
        stats = sb("stats", [P, TQ, 6])
        mv = sb("mv", [P, TQ, 2])
        var_eps = sb("var_eps", [P, TQ])
        rstd = sb("rstd", [P, TQ])
        xn = sb("xn", [P, TQ, D])
        base = sb("base", [P, 2, TQ, D])
        xT_hi = sb("xT_hi", [P, 2, TILE], FP32R)
        xT_lo = sb("xT_lo", [P, 2, TILE], FP32R)
        r1 = sb("r1", [P, TILE])
        lg = sb("lg", [P, TQ, E])
        lmax = sb("lmax", [P, TQ])
        lgd = sb("lgd", [P, TQ, E])
        above = sb("above", [P, TQ, E, E])
        level = sb("level", [P, TQ, E, E])
        rank = sb("rank", [P, TQ, E])
        sel4 = sb("sel4", [P, TQ, E])
        seld = sb("seld", [P, TQ, E])
        ssum = sb("ssum", [P, TQ])
        tin = sb("tin", [P, TQ, E])
        th = sb("th", [P, TQ, E])
        gate = sb("gate", [P, TQ, E])
        rest = sb("rest", [P, TQ, E])
        parts = sb("parts", [P, TQ, SPLITS * E], BF16)
        gateT = sb("gateT", [SPLITS * E, TILE], BF16)
        gate_bc = sb("gate_bc", [P, 2, TILE])
        hid = sb("hid", [P, 4, TILE])
        hid_hi = sb("hid_hi", [P, 4, TILE], FP32R)
        hid_lo = sb("hid_lo", [P, 4, TILE], FP32R)
        mix = sb("mix", [P, 2, TILE])
        acc = sb("acc", [P, 2, TILE])

        up_ps = [ps(f"up{i}") for i in range(2)]
        down_ps = [ps(f"down{i}") for i in range(2)]
        gate_ps = ps("gate")
        in_ps = ps("in")
        logit_ps = ps("logit")
        out_ps = ps("out")
        gateT_ps = logit_ps[0:SPLITS * E, 0:TILE // 2].bitcast(BF16)

        x_first, x_rest, rows_in, w_in = sem("x_first"), sem("x_rest"), sem("rows_in"), [sem(f"w_in{e}") for e in range(E)]
        rw_in, rows_t, rows_ready, w_hi, w_lo, w_lo_late, zeroed, sel_ready = (
            sem("rw_in"), sem("rows_t"), sem("rows_ready"), sem("w_hi"), sem("w_lo"), sem("w_lo_late"), sem("zeroed"), sem("sel_ready"))
        later_in = sem("later_in")
        s_stats, s_mv, s_vareps, s_rstd, s_xn, s_xnT, s_xhi, s_xlo = (
            sem("stats"), sem("mv"), sem("vareps"), sem("rstd"), sem("xn"), sem("xnT"), sem("xhi"), sem("xlo"))
        s_r1p, s_r1, s_logit, s_router, s_tanh, s_gateTp, s_gateT = (
            sem("r1p"), sem("r1"), sem("logit"), sem("router"), sem("tanh"), sem("gateTp"), sem("gateT"))
        s_outT, s_xnew, s_stored = sem("outT"), sem("xnew"), sem("stored")
        s_gatep, s_gate, s_down, s_mixed, s_added = sem("gatep"), sem("gate"), sem("down"), sem("mixed"), sem("added")
        s_up, s_silu, s_hi_odd, s_hi_even, s_lo, s_used = sem("up"), sem("silu"), sem("hi_odd"), sem("hi_even"), sem("lo"), sem("used")

        def xcols(tile, q=None):
            if q is None:
                return bass.ds((tile + 1) * TILE, TILE)
            return bass.ds((tile + 1) * TILE + q * D, D)

        extra = 1 if loads else 0

        def wait_expert_split(engine, e):
            if e < EARLY:
                engine.wait_ge(w_lo, e + 1 + extra)
            else:
                engine.wait_ge(w_lo_late, e - EARLY + 1)

        block = ctx.enter_context(nc.Block())

        @block.sync
        def _(sp):
            if loads:
                def load_x(t, s):
                    sp.dma_start(k.x[:, (t + 1) * TILE:(t + 2) * TILE].rearrange("p (q d) -> p q d", q=TQ),
                                 x_in[t]).then_inc(s, 16)
                load_x(0, x_first)
                sp.dma_start(rawr[:, :], loads["rw1"]).then_inc(rw_in, 16)
                sp.dma_start(k.rw2[:, :], loads["rw2"]).then_inc(rw_in, 16)
                for dst, src in loads["rows"]:
                    sp.dma_start(rows[dst], src).then_inc(rows_in, 16)
                sp.dma_start(k.rb2[:, :], loads["rb2"]).then_inc(rows_in, 16)
            for e in range(0 if loads else RAW, E):
                if e >= RAW:
                    wait_expert_split(sp, e - RAW)
                load_expert(nc, sp, k, e, w_in[e])
            if loads:
                for t in range(1, TILES):
                    load_x(t, x_rest)
                wait_expert_split(sp, E - 1)
                for dst, src in loads["later"]:
                    sp.dma_start(dst, src).then_inc(later_in, 16)
                sp.wait_ge(later_in, 16 * len(loads["later"]))
            if out is not None:
                with sp.Fori(0, TILES) as t:
                    sp.wait_ge(s_xnew, t + 3)
                    sp.dma_start(out[bass.ds(t * TILE, TILE), :].rearrange("(q p) d -> p q d", p=P),
                                 k.x[:, bass.ds((t + 1) * TILE, TILE)].rearrange("p (q d) -> p q d", q=TQ)).then_inc(s_stored, 16)
                sp.wait_ge(s_stored, 16 * TILES)

        @block.tensor
        def _(pe):
            def xn_transpose(n):
                pe.wait_ge(s_xn, n)
                for q in range(TQ):
                    last = nc.tensor.transpose(in_ps[:, q * P:(q + 1) * P], xn[:, q, :], k.ident[:, :])
                last.then_inc(s_xnT, 1)

            def router_hidden(n, b):
                pe.wait_ge(s_xlo, n)
                nc.tensor.matmul(in_ps[:, :], k.rw1_hi[:, :], xT_hi[:, b, :], start=True, stop=False)
                nc.tensor.matmul(in_ps[:, :], k.rw1_hi[:, :], xT_lo[:, b, :], start=False, stop=False)
                nc.tensor.matmul(in_ps[:, :], k.rw1_lo[:, :], xT_hi[:, b, :], start=False, stop=True).then_inc(s_r1p, 1)

            def logits(n):
                pe.wait_ge(s_r1, n)
                for q in range(TQ):
                    last = nc.tensor.matmul(logit_ps[:, q * E:(q + 1) * E], r1[:, q * P:(q + 1) * P], k.rw2[:, :],
                                            start=True, stop=True)
                last.then_inc(s_logit, 1)

            def gate_transpose(router_done):
                pe.wait_ge(s_router, router_done)
                for q in range(TQ):
                    last = nc.tensor.transpose(gateT_ps[:, q * P:(q + 1) * P], parts[:, q, :], k.ident_bf[:, :])
                last.then_inc(s_gateTp, 1)

            def gate_broadcast(e):
                nc.tensor.matmul(gate_ps[:, :], k.sel[:, e, :], gateT[:, :], start=True, stop=True).then_inc(s_gatep, 1)

            def up(j, b):
                e, c = (j % CH) // HC, j % HC
                u = up_ps[j % 2]
                w = slice(c * P, (c + 1) * P)
                nc.tensor.matmul(u[:, :], w1_hi[:, e, w], xT_hi[:, b, :], start=True, stop=False)
                nc.tensor.matmul(u[:, :], w1_hi[:, e, w], xT_lo[:, b, :], start=False, stop=False)
                nc.tensor.matmul(u[:, :], w1_lo[:, e, w], xT_hi[:, b, :], start=False, stop=True).then_inc(s_up, 1)

            def down(j):
                e, c = j // HC, j % HC
                o = down_ps[e % 2]
                nc.tensor.matmul(o[:, :], w2_hi[:, e, c, :], hid_hi[:, c, :], start=(c == 0), stop=False)
                nc.tensor.matmul(o[:, :], w2_hi[:, e, c, :], hid_lo[:, c, :], start=False, stop=False)
                last = nc.tensor.matmul(o[:, :], w2_lo[:, e, c, :], hid_hi[:, c, :], start=False, stop=(c == HC - 1))
                last.then_inc(s_used, 1)

            pe.sem_inc(s_used, 4)
            if loads:
                pe.wait_ge(zeroed, k.n_zeroed)
                pe.wait_ge(rows_in, 16 * (len(loads["rows"]) + 1))
                nc.tensor.transpose(out_ps[:, 0:ROWS], rows[:, :], k.ident[0:ROWS, 0:ROWS]).then_inc(rows_t, 1)
                pe.wait_ge(rows_ready, 1)
            xn_transpose(1)
            if loads:
                pe.wait_ge(w_lo, 1)
            router_hidden(1, 0)
            wait_expert_split(pe, 0)
            up(0, 0)
            up(1, 0)
            if loads:
                pe.wait_ge(rw_in, 32)
            logits(1)
            for j in range(2, AHEAD):
                pe.wait_ge(s_silu, j - 1)
                up(j, 0)
            gate_transpose(RS)
            pe.wait_ge(s_gateT, 1)
            if loads:
                pe.wait_ge(sel_ready, k.n_sel)
            gate_broadcast(0)

            with pe.Fori(0, TILES // UNROLL) as it:
                chunks, tiles, experts = pe.snap(it * (2 * CH)), pe.snap(it * 2), pe.snap(it * (2 * E))
                routed, added = pe.snap(it * (2 * RS)), pe.snap(it * (2 * (E - 1)))
                for b in range(UNROLL):
                    for j in range(CH):
                        e, c = j // HC, j % HC
                        g = b * CH + j
                        if c == 3:
                            pe.wait_ge(s_gate, experts + (b * E + e + 1))
                            if e == E - 1:
                                pe.wait_ge(s_gateT, tiles + (b + 2))
                            gate_broadcast((e + 1) % E)
                        if j == 3:
                            pe.wait_ge(s_added, added + (b * (E - 1) + 1))
                            pe.wait_ge(s_xnew, tiles + (b + 1))
                            for q in range(TQ):
                                last = nc.tensor.transpose(out_ps[:, q * P:(q + 1) * P], acc[:, 1 - b, q * P:(q + 1) * P],
                                                           k.ident[:, :])
                            last.then_inc(s_outT, 1)
                        if j == 6:
                            xn_transpose(tiles + (b + 2))
                        if j == 10:
                            router_hidden(tiles + (b + 2), 1 - b)
                        if j == 14:
                            logits(tiles + (b + 2))
                        if j == 29:
                            gate_transpose(routed + (b + 2) * RS)
                        pe.wait_ge(s_lo, chunks + (g + 1))
                        if c == 0:
                            pe.wait_ge(s_mixed, experts + (b * E + e + 1))
                        down(j)
                        pe.wait_ge(s_silu, chunks + (g + AHEAD - 1))
                        if b == 0 and j + AHEAD < CH and (j + AHEAD) % HC == 0:
                            wait_expert_split(pe, (j + AHEAD) // HC)
                        up(j + AHEAD, b if j + AHEAD < CH else 1 - b)
            pe.wait_ge(s_added, TILES * (E - 1) + 1)
            pe.wait_ge(s_xnew, TILES + 1)
            for q in range(TQ):
                last = nc.tensor.transpose(out_ps[:, q * P:(q + 1) * P], acc[:, 1, q * P:(q + 1) * P], k.ident[:, :])
            last.then_inc(s_outT, 1)

        @block.scalar
        def _(act):
            def x_hi(n, b):
                act.wait_ge(s_xnT, n)
                nc.scalar.activation(xT_hi[:, b, :], in_ps[:, :], ACT.Copy).then_inc(s_xhi, 1)

            def router_silu(n):
                act.wait_ge(s_r1p, n)
                nc.scalar.activation(r1[:, :], in_ps[:, :], ACT.Silu,
                                     bias=k.cols[:, ROW_RB1:ROW_RB1 + 1]).then_inc(s_r1, 1)

            def router_tanh(step12):
                act.wait_ge(s_router, step12)
                nc.scalar.activation(th[:, :, :], tin[:, :, :], ACT.Tanh).then_inc(s_tanh, 1)

            def gate_transposed(n):
                act.wait_ge(s_gateTp, n)
                nc.scalar.activation(gateT[:, :], gateT_ps, ACT.Copy).then_inc(s_gateT, 1)

            def gate_copy(e, n):
                act.wait_ge(s_gatep, n)
                nc.scalar.activation(gate_bc[:, e % 2, :], gate_ps[:, :], ACT.Copy).then_inc(s_gate, 1)

            def silu(j, n):
                e, c = (j % CH) // HC, j % HC
                act.wait_ge(s_up, n)
                col = ROW_BE1 + e * HC + c
                nc.scalar.activation(hid[:, c, :], up_ps[j % 2][:, :], ACT.Silu,
                                     bias=k.cols[:, col:col + 1]).then_inc(s_silu, 1)

            def hid_high_odd(c, n):
                act.wait_ge(s_silu, n)
                nc.scalar.activation(hid_hi[:, c, :], hid[:, c, :], ACT.Copy).then_inc(s_hi_odd, 1)

            if loads:
                act.wait_ge(rw_in, 32)
                nc.scalar.activation(k.rw1_hi[:, :], rawr[:, :], ACT.Copy).then_inc(w_hi, 1)
            def expert_high(e):
                if loads or e >= RAW:
                    act.wait_ge(w_in[e], 32)
                nc.scalar.activation(w1_hi[:, e, :], k.raw1[:, e % RAW, :], ACT.Copy)
                nc.scalar.activation(w2_hi[:, e, :, :], k.raw2[:, e % RAW, :, :], ACT.Copy).then_inc(w_hi, 1)

            expert_high(0)
            x_hi(1, 0)
            expert_high(1)
            if loads:
                act.wait_ge(rows_ready, 1)
            router_silu(1)
            silu(0, 1)
            expert_high(2)
            silu(1, 2)
            expert_high(3)
            expert_high(4)
            router_tanh(12)
            silu(2, 3)
            hid_high_odd(1, 2)
            expert_high(5)
            gate_transposed(1)
            silu(3, 4)
            gate_copy(0, 1)
            for e in range(6, E):
                expert_high(e)

            with act.Fori(0, TILES // UNROLL) as it:
                chunks, tiles, experts = act.snap(it * (2 * CH)), act.snap(it * 2), act.snap(it * (2 * E))
                routed = act.snap(it * (2 * RS))
                for b in range(UNROLL):
                    for j in range(CH):
                        e, c = j // HC, j % HC
                        g = b * CH + j
                        if c % 2 == 0:
                            act.wait_ge(s_used, chunks + (g + 4))
                            hid_high_odd((j + 3) % HC, chunks + (g + 4))
                        act.wait_ge(s_lo, chunks + (g + 1))
                        silu(j + AHEAD, chunks + (g + AHEAD + 1))
                        if c == 3:
                            act.wait_ge(s_mixed, experts + (b * E + e + 2))
                            gate_copy(e + 1, experts + (b * E + e + 2))
                        if j == 7:
                            x_hi(tiles + (b + 2), 1 - b)
                        if j == 11:
                            router_silu(tiles + (b + 2))
                        if j == 23:
                            router_tanh(routed + (b + 1) * RS + 12)
                        if j == 29:
                            gate_transposed(tiles + (b + 2))

        @block.gpsimd
        def _(pool):
            if loads:
                k.make_constants(nc, pool, zeroed)
                pool.wait_ge(zeroed, k.n_zeroed)
            nc.gpsimd.memset(acc[:, 1, :], 0.0).then_inc(s_added, 1)

            def inverse_std(n):
                pool.wait_ge(s_mv, n)
                nc.gpsimd.tensor_tensor(var_eps[:, :], mv[:, :, 1], k.eps[:, 0:TQ], ALU.add).then_inc(s_vareps, 1)
                pool.wait_ge(s_vareps, n)
                nc.gpsimd.tensor_tensor(rstd[:, :], var_eps[:, :], k.minus_half[:, 0:TQ], ALU.pow).then_inc(s_rstd, 1)

            inverse_std(1)
            if loads:
                k.make_select(nc, pool, sel_ready)
            nc.gpsimd.memset(base[:, 1, :, :], 0.0).then_inc(s_xnew, 1)
            for e in range(EARLY, E):
                pool.wait_ge(w_hi, e + 1 + extra)
                nc.gpsimd.tensor_tensor(w1_lo[:, e, :], k.raw1[:, e % RAW, :], w1_hi[:, e, :].bitcast(FP32), ALU.subtract)
                nc.gpsimd.tensor_tensor(w2_lo[:, e, :, :], k.raw2[:, e % RAW, :, :], w2_hi[:, e, :, :].bitcast(FP32),
                                        ALU.subtract).then_inc(w_lo_late, 1)
            with pool.Fori(0, TILES // UNROLL) as it:
                tiles, experts, added = pool.snap(it * 2), pool.snap(it * (2 * E)), pool.snap(it * (2 * (E - 1)))
                for b in range(UNROLL):
                    inverse_std(tiles + (b + 2))
                    for e in range(1, E):
                        pool.wait_ge(s_mixed, experts + (b * E + e + 3))
                        pool.wait_ge(s_added, added + (b * (E - 1) + e))
                        nc.gpsimd.tensor_tensor(acc[:, b, :], acc[:, b, :], mix[:, e % 2, :], ALU.add).then_inc(s_added, 1)

        @block.vector
        def _(dve):
            v = nc.vector

            def stats_of(tile, q):
                return v.bn_stats(stats[:, q, :], k.x[:, xcols(tile, q)])

            def aggregate():
                for q in range(TQ):
                    last = v.bn_aggr(mv[:, q, :], stats[:, q, :])
                last.then_inc(s_mv, 1)

            def normalise(tile, q):
                return v.tensor_scalar(xn[:, q, :], k.x[:, xcols(tile, q)], mv[:, q, 0:1], rstd[:, q:q + 1],
                                       ALU.subtract, ALU.mult)

            def make_base(tile, n, b):
                dve.wait_ge(s_xn, n)
                v.scalar_tensor_tensor(base[:, b, :, :].rearrange("p q d -> p (q d)"), xn[:, :, :].rearrange("p q d -> p (q d)"), 0.5,
                                       k.x[:, xcols(tile)], ALU.mult, ALU.add)

            def x_lo(n, b):
                dve.wait_ge(s_xhi, n)
                v.tensor_tensor(xT_lo[:, b, :], in_ps[:, :], xT_hi[:, b, :].bitcast(FP32), ALU.subtract).then_inc(s_xlo, 1)

            def bc(ap):
                return ap.unsqueeze(2).broadcast_to([P, TQ, E])

            def router(i, n, r):
                if i >= 2 and i not in (5, 10):
                    dve.wait_ge(s_router, r + (i - 1))
                if i == 1:
                    dve.wait_ge(s_logit, n)
                    ins = v.tensor_tensor(lg[:, :, :], logit_ps[:, 0:TQ * E].rearrange("p (q e) -> p q e", q=TQ),
                                          k.rb2[:, :].unsqueeze(1).broadcast_to([P, TQ, E]), ALU.add)
                if i == 2:
                    ins = v.tensor_reduce(lmax[:, :], lg[:, :, :], AXIS_X, ALU.max)
                if i == 3:
                    ins = v.tensor_tensor(lgd[:, :, :], lg[:, :, :], bc(lmax[:, :]), ALU.subtract)
                mine = lgd[:, :, :].unsqueeze(3).broadcast_to([P, TQ, E, E])
                others = lgd[:, :, :].unsqueeze(2).broadcast_to([P, TQ, E, E])
                if i == 4:
                    ins = v.tensor_tensor(above[:, :, :, :], others, mine, ALU.is_gt)
                if i == 5:
                    ins = v.tensor_tensor(level[:, :, :, :], others, mine, ALU.is_equal)
                if i == 6:
                    ins = v.tensor_tensor(level[:, :, :, :], level[:, :, :, :],
                                          k.earlier[:, :, :].unsqueeze(1).broadcast_to([P, TQ, E, E]), ALU.mult)
                if i == 7:
                    ins = v.tensor_tensor(above[:, :, :, :], above[:, :, :, :], level[:, :, :, :], ALU.add)
                if i == 8:
                    ins = v.tensor_reduce(rank[:, :, :], above[:, :, :, :], AXIS_X, ALU.add)
                if i == 9:
                    ins = v.tensor_scalar(sel4[:, :, :], rank[:, :, :], 1.5, 0.25, ALU.is_lt, ALU.mult)
                if i == 10:
                    dve.wait_ge(s_router, r + 9)
                    ins = v.tensor_tensor(seld[:, :, :], sel4[:, :, :], lgd[:, :, :], ALU.mult)
                if i == 11:
                    ins = v.tensor_reduce(ssum[:, :], seld[:, :, :], AXIS_X, ALU.add)
                if i == 12:
                    ins = v.scalar_tensor_tensor(tin[:, :, :], bc(ssum[:, :]), -2.0, lgd[:, :, :], ALU.mult, ALU.add)
                if i == 13:
                    dve.wait_ge(s_tanh, n)
                    ins = v.scalar_tensor_tensor(gate[:, :, :], th[:, :, :], 1.0, sel4[:, :, :], ALU.add, ALU.mult)
                if i == 14:
                    ins = v.tensor_copy(parts[:, :, 0:E], gate[:, :, :])
                if i == 15:
                    ins = v.tensor_tensor(rest[:, :, :], gate[:, :, :], parts[:, :, 0:E], ALU.subtract)
                if i == 16:
                    ins = v.tensor_copy(parts[:, :, E:2 * E], rest[:, :, :])
                if i == 17:
                    ins = v.tensor_tensor(parts[:, :, 2 * E:3 * E], rest[:, :, :], parts[:, :, E:2 * E], ALU.subtract)
                ins.then_inc(s_router, 1)

            def hid_high(c, n):
                dve.wait_ge(s_silu, n)
                dve.wait_ge(s_used, n)
                v.tensor_copy(hid_hi[:, c, :], hid[:, c, :]).then_inc(s_hi_even, 1)

            def hid_low(c, n_high):
                dve.wait_ge(s_hi_odd if c % 2 else s_hi_even, n_high)
                v.tensor_tensor(hid_lo[:, c, :], hid[:, c, :], hid_hi[:, c, :].bitcast(FP32), ALU.subtract).then_inc(s_lo, 1)

            def add_out(tile, n, b):
                dve.wait_ge(s_outT, n)
                v.tensor_tensor(k.x[:, xcols(tile)], out_ps[:, :], base[:, b, :, :].rearrange("p q d -> p (q d)"), ALU.add).then_inc(s_xnew, 1)

            dve.sem_inc(s_mixed, 2)
            if loads:
                dve.wait_ge(x_first, 16)
            for q in range(TQ):
                last = stats_of(0, q)
            last.then_inc(s_stats, 1)
            dve.wait_ge(s_stats, 1)
            aggregate()
            def expert_low(e):
                dve.wait_ge(w_hi, e + 1 + extra)
                v.tensor_tensor(w1_lo[:, e, :], k.raw1[:, e % RAW, :], w1_hi[:, e, :].bitcast(FP32), ALU.subtract)
                v.tensor_tensor(w2_lo[:, e, :, :], k.raw2[:, e % RAW, :, :], w2_hi[:, e, :, :].bitcast(FP32),
                                ALU.subtract).then_inc(w_lo, 1)

            dve.wait_ge(s_rstd, 1)
            for q in range(TQ):
                last = normalise(0, q)
            last.then_inc(s_xn, 1)
            if loads:
                dve.wait_ge(rows_t, 1)
                v.tensor_copy(k.cols[:, :], out_ps[:, 0:ROWS]).then_inc(rows_ready, 1)
                dve.wait_ge(zeroed, k.n_zeroed)
                dve.wait_ge(w_hi, 1)
                v.tensor_tensor(k.rw1_lo[:, :], rawr[:, :], k.rw1_hi[:, :].bitcast(FP32), ALU.subtract).then_inc(w_lo, 1)
            expert_low(0)
            x_lo(1, 0)
            make_base(0, 1, 0)
            expert_low(1)
            for i in range(1, 13):
                router(i, 1, 0)
            expert_low(2)
            for i in range(13, RS + 1):
                router(i, 1, 0)
            hid_high(0, 1)
            hid_low(0, 1)
            hid_high(2, 3)
            hid_low(1, 1)
            if loads:
                dve.wait_ge(x_rest, 16 * (TILES - 1))

            with dve.Fori(0, TILES // UNROLL) as it:
                chunks, tiles, experts = dve.snap(it * (2 * CH)), dve.snap(it * 2), dve.snap(it * (2 * E))
                highs, routed, added = dve.snap(it * CH), dve.snap(it * (2 * RS)), dve.snap(it * (2 * (E - 1)))
                for b in range(UNROLL):
                    nxt = b + 2
                    for j in range(CH):
                        e, c = j // HC, j % HC
                        g = b * CH + j
                        if j == 0:
                            stats_of(tiles + (b + 1), 0)
                            stats_of(tiles + (b + 1), 1)
                        if j == 2:
                            dve.wait_ge(s_stats, tiles + nxt)
                        if j == 4:
                            dve.wait_ge(s_rstd, tiles + nxt)
                            normalise(tiles + (b + 1), 0)
                            normalise(tiles + (b + 1), 1)
                        if j == 8:
                            x_lo(tiles + nxt, 1 - b)
                        if j in ROUTER_BEFORE:
                            router(ROUTER_BEFORE[j], tiles + nxt, routed + (b + 1) * RS)
                        jh, jl = g + 3, g + 2
                        if jh % 2 == 0:
                            hid_high(jh % HC, chunks + (jh + 1))
                        hid_low(jl % HC, highs + (jl // 2 + 1))
                        if j == 0:
                            stats_of(tiles + (b + 1), 2)
                            stats_of(tiles + (b + 1), 3).then_inc(s_stats, 1)
                        if j == 2:
                            aggregate()
                        if j == 4:
                            normalise(tiles + (b + 1), 2)
                            normalise(tiles + (b + 1), 3).then_inc(s_xn, 1)
                        if j == 6:
                            add_out(tiles + (b - 1), tiles + (b + 1), 1 - b)
                        if j == 10:
                            make_base(tiles + (b + 1), tiles + nxt, 1 - b)
                        if j in ROUTER_AFTER:
                            router(ROUTER_AFTER[j], tiles + nxt, routed + (b + 1) * RS)
                        if c == HC - 1:
                            dve.wait_ge(s_used, chunks + (g + 1 + 4))
                            dve.wait_ge(s_gate, experts + (b * E + e + 1))
                            if e == 0:
                                to = acc[:, b, :]
                            else:
                                to = mix[:, e % 2, :]
                                prior = b * (E - 1) + max(e - 2, 0) + 1
                                dve.wait_ge(s_added, added + prior)
                            col = ROW_BE2 + e
                            v.scalar_tensor_tensor(to, down_ps[e % 2][:, :], k.cols[:, col:col + 1], gate_bc[:, e % 2, :],
                                                   ALU.add, ALU.mult).then_inc(s_mixed, 1)
            add_out(TILES - 1, TILES + 1, 1)



def attention_phase(nc, k, out=None):
    NB = k.tiles * TILE // BT
    DH = 64
    UNITS = 4
    FILLS = 11
    PAIRS = AH // P
    QKRING = 4
    NRING = 4
    BQ = BT // P
    name = "at"
    with ExitStack() as ctx:
        def sb(n, shape, dt=FP32):
            return ctx.enter_context(nc.sbuf_tensor(f"{name}_{n}", shape, dt))

        def ps(n):
            return ctx.enter_context(nc.psum_tensor(f"{name}_{n}_ps", [P, 512], FP32))

        def sem(n):
            return ctx.enter_context(nc.semaphore(f"{name}_{n}_sem"))

        wq_hi, wk_hi, wv_hi = [sb(f"w{n}_hi", [P, AH], FP32R) for n in "qkv"]
        wq_lo, wk_lo, wv_lo = [sb(f"w{n}_lo", [P, AH], FP32R) for n in "qkv"]
        wf1_hi, wf1_lo = sb("wf1_hi", [P, HID], FP32R), sb("wf1_lo", [P, HID], FP32R)
        mask = sb("mask", [P, 3, P])
        den_sel = sb("den_sel", [P, UNITS, 32])
        wo_hi, wo_lo = sb("wo_hi", [P, PAIRS, D], FP32R), sb("wo_lo", [P, PAIRS, D], FP32R)
        head_sel = sb("head_sel", [P, PAIRS, P], FP32R)
        st = {n: sb(f"stats_{n}", [P, BQ, 6]) for n in "ABC"}
        mv = {n: sb(f"mv_{n}", [P, BQ, 2]) for n in "ABC"}
        ve = {n: sb(f"ve_{n}", [P, BQ]) for n in "ABC"}
        rs = {n: sb(f"rs_{n}", [P, BQ]) for n in "ABC"}
        y = sb("y", [P, NRING, BQ, D])
        z = sb("z", [P, BQ, D])
        hT = sb("hT", [P, BT])
        hT_hi, hT_lo = sb("hT_hi", [P, 2, BT], FP32R), sb("hT_lo", [P, 2, BT], FP32R)
        exps, relus = sb("exps", [P, 2, 2 * BT]), sb("relus", [P, 2, 2 * BT])
        qk = sb("qk", [P, QKRING, 2, BT])
        qk_hi, qk_lo = sb("qk_hi", [P, QKRING, BT + P], FP32R), sb("qk_lo", [P, QKRING, BT + P], FP32R)
        vals = sb("vals", [P, 2, BQ, AH // 2])
        sc = sb("sc", [P, 2, 4, 4, P])
        head_sel_f = sc[:, 1, :, :, :].rearrange("p a b n -> p (a b n)")[:, 0:AH].rearrange("p (c h d) -> p c h d", c=PAIRS, h=2)
        num = sb("num", [P, UNITS, 2 * BT])
        o_hi, o_lo = sb("o_hi", [P, UNITS, 2 * BT], FP32R), sb("o_lo", [P, UNITS, 2 * BT], FP32R)
        den = sb("den", [P, BT])
        rden = sb("rden", [P, BT])
        rden_hi, rden_parts = sb("rden_hi", [P, BT], FP32R), sb("rden_parts", [P, BT], FP32R)
        low_rows_4, low_rows = sb("low_rows_4", [P, 4]), sb("low_rows", [P, 1])
        attnT = sb("attnT", [P, BT])
        a_nat = sb("a_nat", [P, BQ, D])
        xa = sb("xa", [P, BQ, D])
        an = sb("an", [P, BQ, D])
        h2 = sb("h2", [P, BT])
        h2_hi, h2_lo = sb("h2_hi", [P, BT], FP32R), sb("h2_lo", [P, BT], FP32R)
        gel = sb("gel", [P, HC, BT])
        warm = sb("warm", [P, 2])

        s_ps = [ps(f"s{i}") for i in range(4)]
        proj_ps, num_ps, den_ps, slot_ps = ps("proj"), ps("num"), ps("den"), ps("slot")

        s_split_hi, s_split_lo, s_const, s_head_sel, w_next, s_zero = (
            sem("split_hi"), sem("split_lo"), sem("const"), sem("head_sel"), sem("w_next"), sem("zero"))
        s_stored = sem("stored")
        s_st = {n: sem(f"st{n}") for n in "ABC"}
        s_mv = {n: sem(f"mv{n}") for n in "ABC"}
        s_ve = {n: sem(f"ve{n}") for n in "ABC"}
        s_rs = {n: sem(f"rs{n}") for n in "ABC"}
        s_y, s_z, s_hT, s_hT_hi, s_hT_lo = sem("y"), sem("z"), sem("hT"), sem("hT_hi"), sem("hT_lo")
        s_proj, s_proj_out, s_exp, s_phi = sem("proj"), sem("proj_out"), sem("exp"), sem("phi")
        s_qk_hi, s_qk_lo = sem("qk_hi"), sem("qk_lo")
        s_score, s_masked, s_quad, s_num, s_num_out = sem("score"), sem("masked"), sem("quad"), sem("num"), sem("num_out")
        s_den, s_rden, s_rhi, s_rparts = sem("den"), sem("rden"), sem("rhi"), sem("rparts")
        s_low_rows = sem("low_rows")
        s_slot = sem("slot")
        s_o_hi, s_o_lo, s_sum = sem("o_hi"), sem("o_lo"), sem("sum")
        s_o, s_attnT, s_a, s_xa, s_an, s_h2, s_h2_hi, s_h2_lo, s_gelu, s_x = (
            sem("o"), sem("attnT"), sem("a"), sem("xa"), sem("an"), sem("h2"), sem("h2_hi"), sem("h2_lo"),
            sem("gelu"), sem("x"))

        fills_before = (0, 2, 5, 8)
        first_banks = [proj_ps, s_ps[0], s_ps[1], s_ps[2]]
        first_fills = [("qk", 0), ("qk", 1), ("v", 0), ("qk", 2), ("qk", 3), ("v", 1)]

        def xc(s, q=None):
            if q is None:
                return bass.ds((s + 2) * BT, BT)
            return bass.ds((s + 2) * BT + q * D, D)

        def flat(ap):
            return ap.rearrange("p a b -> p (a b)")

        block = ctx.enter_context(nc.Block())

        @block.sync
        def _(sp):
            sp.wait_ge(s_split_lo, 4)
            for e in range(RAW):
                load_expert(nc, sp, k, e, w_next)
            if out is not None:
                with sp.Fori(0, NB) as s:
                    sp.wait_ge(s_x, s + 3)
                    sp.dma_start(out[bass.ds(s * BT, BT), :].rearrange("(q p) d -> p q d", p=P),
                                 k.x[:, bass.ds((s + 2) * BT, BT)].rearrange("p (q d) -> p q d", q=BQ)).then_inc(s_stored, 16)
                sp.wait_ge(s_stored, 16 * NB)
            sp.wait_ge(w_next, 32 * RAW)

        @block.tensor
        def _(pe):
            mm = nc.tensor.matmul

            def transpose_slot(src, bank=slot_ps):
                for q in range(BQ):
                    last = nc.tensor.transpose(bank[:, q * P:(q + 1) * P], src(q), k.ident[:, :])
                last.then_inc(s_slot, 1)

            def ffn_up(c0, bank=slot_ps):
                for i in range(2):
                    o, w = bank[:, i * BT:(i + 1) * BT], slice((c0 + i) * P, (c0 + i + 1) * P)
                    mm(o, wf1_hi[:, w], h2_hi[:, :], start=True, stop=False)
                    mm(o, wf1_hi[:, w], h2_lo[:, :], start=False, stop=False)
                    last = mm(o, wf1_lo[:, w], h2_hi[:, :], start=False, stop=True)
                last.then_inc(s_slot, 1)

            def ffn_down():
                for q in range(BQ):
                    t = slice(q * P, (q + 1) * P)
                    for c in range(HC):
                        last = mm(slot_ps[:, t], gel[:, c, t], k.wf2[:, c, :], start=(c == 0), stop=(c == HC - 1))
                last.then_inc(s_slot, 1)

            def broadcast(i, bank=slot_ps):
                for cc in range(2):
                    o, sel = bank[:, cc * BT:(cc + 1) * BT], head_sel[:, 2 * i + cc, :]
                    last = mm(o, sel, rden_parts[:, :], start=True, stop=True)
                last.then_inc(s_slot, 1)

            def output_product(n):
                for c in range(PAIRS):
                    if c % 2 == 0:
                        pe.wait_ge(s_o_lo, n + (c // 2 + 1))
                    cols = slice((c % 2) * BT, (c % 2 + 1) * BT)
                    hi, lo = o_hi[:, c // 2, cols], o_lo[:, c // 2, cols]
                    mm(slot_ps[:, 0:BT], wo_hi[:, c, :], hi, start=(c == 0), stop=False)
                    mm(slot_ps[:, 0:BT], wo_hi[:, c, :], lo, start=False, stop=False)
                    last = mm(slot_ps[:, 0:BT], wo_lo[:, c, :], hi, start=False, stop=(c == PAIRS - 1))
                last.then_inc(s_slot, 1)

            def project_qk(c, b, bank):
                w = slice(c * P, (c + 1) * P)
                for i, (hi, lo) in enumerate(((wq_hi, wq_lo), (wk_hi, wk_lo))):
                    o = bank[:, i * BT:(i + 1) * BT]
                    mm(o, hi[:, w], hT_hi[:, b, :], start=True, stop=False)
                    mm(o, hi[:, w], hT_lo[:, b, :], start=False, stop=False)
                    last = mm(o, lo[:, w], hT_hi[:, b, :], start=False, stop=True)
                last.then_inc(s_proj, 1)

            def project_v(half, q, b, bank):
                t, w = slice(q * P, (q + 1) * P), slice(half * AH // 2, (half + 1) * AH // 2)
                mm(bank[:, :], hT_hi[:, b, t], wv_hi[:, w], start=True, stop=False)
                mm(bank[:, :], hT_lo[:, b, t], wv_hi[:, w], start=False, stop=False)
                mm(bank[:, :], hT_hi[:, b, t], wv_lo[:, w], start=False, stop=True).then_inc(s_proj, 1)

            def scores(c):
                i = c % QKRING
                q, k1 = slice(0, BT), slice(BT, BT + P)
                for half in range(2):
                    r, o = slice(half * DH, (half + 1) * DH), s_ps[2 * (c % 2) + half]
                    mm(o[:, 0:BT], qk_hi[r, i, k1], qk_hi[r, i, q], start=True, stop=False)
                    mm(o[:, 0:BT], qk_hi[r, i, k1], qk_lo[r, i, q], start=False, stop=False)
                    mm(o[:, 0:BT], qk_lo[r, i, k1], qk_hi[r, i, q], start=False, stop=True)
                for half in range(2):
                    r, o = slice(half * DH, (half + 1) * DH), s_ps[2 * (c % 2) + half]
                    last = mm(o[:, BT:BT + P], qk[r, i, 1, P:BT], qk[r, i, 0, P:BT], start=True, stop=True)
                last.then_inc(s_score, 1)

            def values(u):
                for cc in range(2):
                    o = num_ps[:, cc * BT:(cc + 1) * BT]
                    for half in range(2):
                        h = (4 * u + 2 * cc + half) % 8
                        v = slice(h * DH, (h + 1) * DH)
                        r, s4 = slice(half * DH, (half + 1) * DH), sc[:, u % 2, 2 * cc + half, :, :]
                        mm(o[r, :], vals[:, u // 2, 0, v], flat(s4[:, 0:2, :]), start=True, stop=False)
                    for half in range(2):
                        h = (4 * u + 2 * cc + half) % 8
                        v = slice(h * DH, (h + 1) * DH)
                        r, s4 = slice(half * DH, (half + 1) * DH), sc[:, u % 2, 2 * cc + half, :, :]
                        last = mm(o[r, P:BT], vals[:, u // 2, 1, v], s4[:, 2, :], start=False, stop=True)
                last.then_inc(s_num, 1)

            def denominators(u):
                for j in range(4):
                    last = mm(den_ps[32 * j:32 * j + 32, 0:BT], den_sel[:, u, :], sc[:, u % 2, j, 0:4:3, :],
                              start=(u == 0), stop=(u == UNITS - 1))
                last.then_inc(s_quad, 1)

            pe.sem_inc(s_quad, 1)
            pe.wait_ge(s_z, 1)
            transpose_slot(lambda q: z[:, q, :])
            pe.wait_ge(s_hT_lo, 1)
            for n, (what, i) in enumerate(first_fills):
                if n >= len(first_banks):
                    pe.wait_ge(s_proj_out, n - len(first_banks) + 1)
                bank = first_banks[n % len(first_banks)]
                if what == "qk":
                    if i == 0:
                        pe.wait_ge(s_split_lo, 2)
                    project_qk(i, 0, bank)
                else:
                    if i == 0:
                        pe.wait_ge(s_split_lo, 3)
                    project_v(0, i, 0, bank)
            pe.wait_ge(s_z, 2)
            pe.wait_ge(s_hT, 1)
            transpose_slot(lambda q: z[:, q, :])
            pe.wait_ge(s_proj_out, len(first_fills))
            for cc in range(2):
                pe.wait_ge(s_qk_lo, cc + 1)
                scores(cc)
            pe.wait_ge(s_split_lo, 4)
            pe.wait_ge(s_const, k.n_attn_const)
            pe.wait_ge(s_head_sel, 1)
            pe.wait_ge(s_zero, 4)

            with pe.Fori(0, NB // NRING) as it:
                ones, twos, fours, eights, twelves = (pe.snap(it * (NRING * m)) for m in (1, 2, 4, 8, 12))
                for b in range(NRING):
                    for u in range(UNITS):
                        proj = twelves + (12 * b + 3 * u + len(first_fills))
                        for cc in range(2):
                            pe.wait_ge(s_qk_lo, eights + (8 * b + 2 * (u + 1) + cc + 1))
                            pe.wait_ge(s_masked, eights + (8 * b + 2 * u + cc + 1))
                            scores((2 * (u + 1) + cc) % PAIRS)
                            if (u, cc) == (2, 0):
                                pe.wait_ge(s_hT_lo, ones + (b + 2))
                            pe.wait_ge(s_proj_out, proj + cc)
                            project_qk((2 * (u + 2) + cc) % PAIRS, (b + (u + 2) // UNITS) % 2, proj_ps)
                            if (u, cc) == (0, 0):
                                pe.wait_ge(s_gelu, twos + (2 * b + 2))
                                ffn_down()
                            if (u, cc) == (0, 1):
                                pe.wait_ge(s_rparts, ones + (b + 1))
                                pe.wait_ge(s_x, ones + (b + 1))
                                broadcast(0)
                            if (u, cc) == (1, 0):
                                pe.wait_ge(s_o, fours + (4 * b + 1))
                                broadcast(1)
                            if (u, cc) == (1, 1):
                                pe.wait_ge(s_o, fours + (4 * b + 2))
                                broadcast(2)
                            if (u, cc) == (2, 0):
                                pe.wait_ge(s_o, fours + (4 * b + 4))
                                pe.wait_ge(s_split_lo, 5)
                                output_product(fours + 4 * b)
                            if (u, cc) == (2, 1):
                                pe.wait_ge(s_attnT, ones + (b + 1))
                                transpose_slot(lambda q: attnT[:, q * P:(q + 1) * P])
                            if (u, cc) == (3, 0):
                                pe.wait_ge(s_an, ones + (b + 1))
                                pe.wait_ge(s_hT, ones + (b + 3))
                                transpose_slot(lambda q: an[:, q, :])
                        pe.wait_ge(s_masked, eights + (8 * b + 2 * u + 2))
                        pe.wait_ge(s_num_out, fours + (4 * b + u + 4))
                        if u % 2 == 0:
                            pe.wait_ge(s_proj_out, proj)
                        values(u)
                        if u == 0:
                            pe.wait_ge(s_den, ones + (b + 1))
                        if u == 3:
                            pe.wait_ge(s_h2_lo, ones + (b + 1))
                            ffn_up(0)
                        pe.wait_ge(s_sum, fours + (4 * b + u + 1))
                        denominators(u)
                        pe.wait_ge(s_proj_out, proj + 2)
                        project_v(((u + 2) // 2) % 2, u % 2, (b + (u + 2) // UNITS) % 2, proj_ps)
                        if u == 1:
                            pe.wait_ge(s_o, fours + (4 * b + 3))
                            broadcast(3)
                        if u == 2:
                            pe.wait_ge(s_z, ones + (b + 3))
                            pe.wait_ge(s_a, ones + (b + 1))
                            transpose_slot(lambda q: z[:, q, :])
                        if u == 3:
                            pe.wait_ge(s_gelu, twos + (2 * b + 3))
                            ffn_up(2)
            pe.wait_ge(s_gelu, 2 * NB + 2)
            ffn_down()
            pe.wait_ge(s_rparts, NB + 1)
            pe.wait_ge(s_masked, 8 * NB + 2)
            for i in range(UNITS):
                broadcast(i, s_ps[i])
            pe.wait_ge(s_x, NB + 1)
            output_product(4 * NB)
            pe.wait_ge(s_attnT, NB + 1)
            transpose_slot(lambda q: attnT[:, q * P:(q + 1) * P])
            pe.wait_ge(s_an, NB + 1)
            transpose_slot(lambda q: an[:, q, :])
            pe.wait_ge(s_h2_lo, NB + 1)
            ffn_up(0, s_ps[0])
            ffn_up(2, s_ps[1])
            pe.wait_ge(s_gelu, 2 * NB + 4)
            ffn_down()

        @block.scalar
        def _(act):
            A = nc.scalar.activation

            def phi_parts(c, n, n_used, bank=proj_ps):
                act.wait_ge(s_proj, n)
                if n_used is not None:
                    act.wait_ge(s_phi, n_used)
                A(exps[:, c % 2, :], bank[:, :], ACT.Exp).then_inc(s_exp, 1)
                A(relus[:, c % 2, :], bank[:, :], ACT.Relu).then_inc(s_proj_out, 1)

            def copy_v(half, q, n, bank=proj_ps):
                act.wait_ge(s_proj, n)
                A(vals[:, half, q, :], bank[:, :], ACT.Copy).then_inc(s_proj_out, 1)

            def affine(dst, g_col, n, s):
                act.wait_ge(s_slot, n)
                A(dst, slot_ps[:, 0:BT], ACT.Identity, bias=k.cols[:, g_col + 1:g_col + 2],
                  scale=k.cols[:, g_col:g_col + 1]).then_inc(s, 1)

            def gelu(c, n, bank=slot_ps):
                act.wait_ge(s_slot, n)
                A(flat(gel[:, c:c + 2, :]), bank[:, :], ACT.Gelu).then_inc(s_gelu, 1)

            act.sem_inc(s_num_out, 4)
            act.sem_inc(s_gelu, 2)
            for raw, hi in zip(k.raw_qkv + [k.raw_f1], (wq_hi, wk_hi, wv_hi, wf1_hi)):
                A(hi[:, :], raw, ACT.Copy).then_inc(s_split_hi, 1)

            def weighted_high(i, n):
                act.wait_ge(s_o, n + (i + 1))
                A(o_hi[:, i, :], num[:, i, :], ACT.Copy).then_inc(s_o_hi, 1)
            affine(hT[:, :], ROW_G1, 1, s_hT)
            for n, (what, i) in enumerate(first_fills):
                bank = first_banks[n % len(first_banks)]
                if what == "qk":
                    phi_parts(i, n + 1, i - 1 if i >= 2 else None, bank)
                else:
                    copy_v(0, i, n + 1, bank)
            act.wait_ge(s_hT_lo, 1)
            affine(hT[:, :], ROW_G1, 2, s_hT)
            A(wo_hi[:, :, :], k.wo[:, :, :], ACT.Copy).then_inc(s_split_hi, 1)
            act.wait_ge(s_zero, 4)

            with act.Fori(0, NB // NRING) as it:
                ones, fours, eights, fills, twelves = (act.snap(it * (NRING * m)) for m in (1, 4, 8, FILLS, 12))
                for b in range(NRING):
                    for u in range(UNITS):
                        fill = fills + (FILLS * b + fills_before[u] + 2)
                        proj = twelves + (12 * b + 3 * u + len(first_fills))
                        for cc in range(2):
                            c = 2 * u + cc
                            phi_parts(c, proj + (cc + 1), eights + (8 * b + c + QKRING - 1))
                            slot = 3 * u + cc
                            if slot in (1, 3):
                                weighted_high(slot // 2, fours + 4 * b)
                            if slot == 6:
                                act.wait_ge(s_slot, fill + 1)
                                A(attnT[:, :], slot_ps[:, 0:BT], ACT.Copy).then_inc(s_attnT, 1)
                            if slot == 9:
                                affine(h2[:, :], ROW_G2, fill + 1, s_h2)
                            if slot == 10:
                                gelu(0, fill + 2)
                        if u == 0:
                            copy_v(1, 0, proj + 3)
                        act.wait_ge(s_num, fours + (4 * b + u + 1))
                        act.wait_ge(s_o_lo, fours + (4 * b + u + 1))
                        A(num[:, u, :], num_ps[:, :], ACT.Copy).then_inc(s_num_out, 1)
                        if u == 1:
                            weighted_high(2, fours + 4 * b)
                        if u > 0:
                            copy_v(((u + 2) // 2) % 2, u % 2, proj + 3)
                        if u == 1:
                            weighted_high(3, fours + 4 * b)
                        if u == 2:
                            affine(hT[:, :], ROW_G1, fill + 3, s_hT)
                        if u == 3:
                            gelu(2, fill + 3)
                            A(warm[:, 0:1], k.minus_half[:, 0:1], ACT.Exp)
            n = 2 + FILLS * NB
            for i in range(UNITS):
                weighted_high(i, 4 * NB)
            A(warm[:, 1:2], k.minus_half[:, 0:1], ACT.Gelu)
            act.wait_ge(s_slot, n + 6)
            A(attnT[:, :], slot_ps[:, 0:BT], ACT.Copy).then_inc(s_attnT, 1)
            affine(h2[:, :], ROW_G2, n + 8, s_h2)
            gelu(0, n + 9, s_ps[0])
            gelu(2, n + 10, s_ps[1])

        @block.gpsimd
        def _(pool):
            g = nc.gpsimd

            def inverse_std(ln, n):
                pool.wait_ge(s_mv[ln], n)
                g.tensor_tensor(ve[ln][:, :], mv[ln][:, :, 1], k.eps[:, 0:BQ], ALU.add).then_inc(s_ve[ln], 1)
                pool.wait_ge(s_ve[ln], n)
                g.tensor_tensor(rs[ln][:, :], ve[ln][:, :], k.minus_half[:, 0:BQ], ALU.pow).then_inc(s_rs[ln], 1)

            def qk_low(c, n):
                pool.wait_ge(s_qk_hi, n)
                g.tensor_tensor(qk_lo[:, c % QKRING, :], flat(qk[:, c % QKRING, :, :])[:, 0:BT + P],
                                qk_hi[:, c % QKRING, :].bitcast(FP32), ALU.subtract).then_inc(s_qk_lo, 1)

            def sum_blocks(par, n):
                pool.wait_ge(s_masked, n)
                g.tensor_tensor(sc[:, par, :, 3, :], sc[:, par, :, 1, :], sc[:, par, :, 2, :], ALU.add).then_inc(s_sum, 1)

            def weighted_low(i, n):
                pool.wait_ge(s_o_hi, n + (i + 1))
                g.tensor_tensor(o_lo[:, i, :], num[:, i, :], o_hi[:, i, :].bitcast(FP32),
                                ALU.subtract).then_inc(s_o_lo, 1)

            inverse_std("A", 1)
            g.memset(gel[:, :, :], 0.0).then_inc(s_zero, 1)
            inverse_std("B", 1)
            inverse_std("A", 2)
            g.memset(xa[:, :, :], 0.0).then_inc(s_xa, 1)
            g.memset(num[:, :, :], 0.0).then_inc(s_zero, 1)
            g.memset(y[:, NRING - 1, :, :], 0.0).then_inc(s_zero, 1)
            g.memset(mask[:, :, :], 1.0).then_inc(s_const, 1)
            g.memset(den_sel[:, :, :], 0.0).then_inc(s_const, 1)
            g.memset(head_sel_f, 0.0).then_inc(s_const, 1)
            g.memset(low_rows_4[:, :], -1.0).then_inc(s_const, 1)
            pool.wait_ge(s_const, 4)
            for blk in (0, 2):
                g.affine_select(out=mask[:, blk, :], in_=mask[:, blk, :], compare_op=ALU.is_ge, fill=0.0, base=0,
                                pattern=[[1, P]], channel_multiplier=-1).then_inc(s_const, 1)
            inverse_std("B", 2)
            qk_low(0, 1)
            g.affine_select(out=low_rows_4[:, :], in_=low_rows_4[:, :], compare_op=ALU.is_ge, fill=0.0, base=-16,
                            pattern=[[-32, 4]], channel_multiplier=1).then_inc(s_const, 1)
            for part in range(2):
                if part:
                    pool.wait_ge(s_const, 10)
                g.affine_select(out=den_sel[:, :, :], in_=den_sel[:, :, :], compare_op=ALU.not_equal, fill=1.0,
                                base=16 * part, pattern=[[1, UNITS], [-1, 32]], channel_multiplier=0).then_inc(s_const, 1)
                for cc in range(2):
                    heads = head_sel_f[:, cc::2, :, :]
                    g.affine_select(out=heads, in_=heads, compare_op=ALU.not_equal, fill=1.0, base=-64 * cc - 16 * part,
                                    pattern=[[-1, UNITS], [-32, 2], [0, DH]], channel_multiplier=1).then_inc(s_const, 1)
            g.affine_select(out=low_rows_4[:, :], in_=low_rows_4[:, :], compare_op=ALU.is_ge, fill=0.0, base=31,
                            pattern=[[32, 4]], channel_multiplier=-1).then_inc(s_const, 1)
            for c in range(1, QKRING):
                qk_low(c, c + 1)
            sum_blocks(0, 2)

            with pool.Fori(0, NB // NRING) as it:
                ones, fours, eights = (pool.snap(it * (NRING * m)) for m in (1, 4, 8))
                for b in range(NRING):
                    for c in range(PAIRS):
                        if c == 1:
                            inverse_std("A", ones + (b + 3))
                            weighted_low(0, fours + 4 * b)
                        if c == 4:
                            inverse_std("B", ones + (b + 3))
                        if c == 5:
                            inverse_std("C", ones + (b + 1))
                        if c == 2:
                            weighted_low(1, fours + 4 * b)
                        if c == 3:
                            weighted_low(2, fours + 4 * b)
                        qk_low(c, eights + (8 * b + c + QKRING + 1))
                        if c == 3:
                            weighted_low(3, fours + 4 * b)
                        if c % 2 == 1:
                            sum_blocks((c // 2 + 1) % 2, eights + (8 * b + c + 3))
            for i in range(UNITS):
                weighted_low(i, 4 * NB)
            inverse_std("C", NB + 1)

        @block.vector
        def _(dve):
            v = nc.vector
            tt, ts, stt = v.tensor_tensor, v.tensor_scalar, v.scalar_tensor_tensor

            def stats(ln, src):
                for q in range(BQ):
                    last = v.bn_stats(st[ln][:, q, :], src(q))
                last.then_inc(s_st[ln], 1)

            def aggregate(ln):
                for q in range(BQ):
                    last = v.bn_aggr(mv[ln][:, q, :], st[ln][:, q, :])
                last.then_inc(s_mv[ln], 1)

            def normalise(ln, n, dst, src, s):
                dve.wait_ge(s_rs[ln], n)
                for q in range(BQ):
                    last = ts(dst(q), src(q), mv[ln][:, q, 0:1], rs[ln][:, q:q + 1], ALU.subtract, ALU.mult)
                last.then_inc(s, 1)

            def split_hT(n, b):
                dve.wait_ge(s_hT, n)
                v.tensor_copy(hT_hi[:, b, :], hT[:, :]).then_inc(s_hT_hi, 1)
                dve.wait_ge(s_hT_hi, n)
                tt(hT_lo[:, b, :], hT[:, :], hT_hi[:, b, :].bitcast(FP32), ALU.subtract).then_inc(s_hT_lo, 1)

            def split_rden():
                stt(rden_parts[:, :], rden_hi[:, :].bitcast(FP32), low_rows[:, 0:1], rden[:, :], ALU.mult,
                    ALU.add).then_inc(s_rparts, 1)

            def phi(c, n_out, n):
                dve.wait_ge(s_proj_out, n_out)
                full = flat(qk[:, c % QKRING, :, :])
                stt(full, exps[:, c % 2, :], 1.0, relus[:, c % 2, :], ALU.min, ALU.add).then_inc(s_phi, 1)
                dve.wait_ge(s_phi, n)
                v.tensor_copy(qk_hi[:, c % QKRING, :], full[:, 0:BT + P]).then_inc(s_qk_hi, 1)

            def mask_scores(cc, par, n):
                dve.wait_ge(s_score, n)
                for half in range(2):
                    last = tt(flat(sc[:, par, 2 * cc + half, 0:3, :]), s_ps[2 * cc + half][:, 0:3 * P], flat(mask[:, :, :]), ALU.mult)
                last.then_inc(s_masked, 1)

            def weigh(i, n, n_num, bank=slot_ps):
                dve.wait_ge(s_slot, n)
                dve.wait_ge(s_num_out, n_num + (i + 1))
                tt(num[:, i, :], num[:, i, :], bank[:, :], ALU.mult).then_inc(s_o, 1)

            v.memset(den_ps[:, 0:BT], 0.0).then_inc(s_zero, 1)
            def low(i):
                raw = (k.raw_qkv + [k.raw_f1])[i]
                hi, lo = ((wq_hi, wq_lo), (wk_hi, wk_lo), (wv_hi, wv_lo), (wf1_hi, wf1_lo))[i]
                dve.wait_ge(s_split_hi, i + 1)
                tt(lo[:, :], raw, hi[:, :].bitcast(FP32), ALU.subtract).then_inc(s_split_lo, 1)

            def first_mean(ln, i, src):
                stats(ln, src)
                dve.wait_ge(s_st[ln], i + 1)
                aggregate(ln)

            def y_of(i):
                return lambda q: y[:, i, q, :]

            def x_of(i):
                return lambda q: k.x[:, xc(i, q)]

            first_mean("A", 0, x_of(0))
            low(0)
            normalise("A", 1, y_of(0), x_of(0), s_y)
            dve.wait_ge(s_y, 1)
            first_mean("B", 0, y_of(0))
            first_mean("A", 1, x_of(1))
            normalise("B", 1, lambda q: z[:, q, :], y_of(0), s_z)
            low(1)
            split_hT(1, 0)
            normalise("A", 2, y_of(1), x_of(1), s_y)
            low(2)
            dve.wait_ge(s_y, 2)
            first_mean("B", 1, y_of(1))
            phi(0, 1, 1)
            phi(1, 2, 2)
            dve.wait_ge(s_slot, 1)
            normalise("B", 2, lambda q: z[:, q, :], y_of(1), s_z)
            low(3)
            phi(2, 4, 3)
            phi(3, 5, 4)
            split_hT(2, 1)
            dve.wait_ge(s_const, 6)
            for cc in range(2):
                mask_scores(cc, 0, cc + 1)
            dve.wait_ge(s_const, k.n_attn_const)
            v.tensor_copy(head_sel[:, :, :], head_sel_f.rearrange("p c h d -> p c (h d)")).then_inc(s_head_sel, 1)
            v.tensor_reduce(low_rows[:, :], low_rows_4[:, :], AXIS_X, ALU.add).then_inc(s_low_rows, 1)
            dve.wait_ge(s_split_hi, 5)
            tt(wo_lo[:, :, :], k.wo[:, :, :], wo_hi[:, :, :].bitcast(FP32), ALU.subtract).then_inc(s_split_lo, 1)
            dve.wait_ge(s_zero, 4)
            dve.wait_ge(s_head_sel, 1)
            dve.wait_ge(s_low_rows, 1)

            with dve.Fori(0, NB // NRING) as it:
                ones, fours, eights, fills, twelves = (dve.snap(it * (NRING * m)) for m in (1, 4, 8, FILLS, 12))
                for b in range(NRING):
                    s = ones + b
                    for u in range(UNITS):
                        fill = fills + (FILLS * b + fills_before[u] + 2)
                        proj = twelves + (12 * b + 3 * u + len(first_fills))
                        if u == 0:
                            dve.wait_ge(s_quad, fours + (4 * b + 1))
                            ts(den[:, :], den_ps[:, 0:BT], EPS_DEN, None, ALU.max).then_inc(s_den, 1)
                        dve.wait_ge(s_quad, fours + (4 * b + u + 1))
                        if u == 0:
                            dve.wait_ge(s_den, ones + (b + 1))
                            v.reciprocal(rden[:, :], den[:, :]).then_inc(s_rden, 1)
                        mask_scores(0, (u + 1) % 2, eights + (8 * b + 2 * u + 3))
                        if u == 0:
                            dve.wait_ge(s_rden, ones + (b + 1))
                            v.tensor_copy(rden_hi[:, :], rden[:, :]).then_inc(s_rhi, 1)
                            stats("A", lambda q: k.x[:, xc(s + 2, q)])
                            dve.wait_ge(s_rhi, ones + (b + 1))
                            split_rden()
                            dve.wait_ge(s_st["A"], ones + (b + 3))
                        if u == 1:
                            weigh(1, fill + 1, fours + 4 * b)
                        if u == 3:
                            dve.wait_ge(s_h2, ones + (b + 1))
                            v.tensor_copy(h2_hi[:, :], h2[:, :]).then_inc(s_h2_hi, 1)
                        phi(2 * u, proj + 1, eights + (8 * b + 2 * u + QKRING + 1))
                        if u == 0:
                            dve.wait_ge(s_slot, fill + 1)
                            dve.wait_ge(s_xa, ones + (b + 1))
                            tt(k.x[:, xc(s - 2)], slot_ps[:, 0:BT], flat(xa[:, :, :]), ALU.add).then_inc(s_x, 1)
                            aggregate("A")
                        if u == 3:
                            dve.wait_ge(s_h2_hi, ones + (b + 1))
                            tt(h2_lo[:, :], h2[:, :], h2_hi[:, :].bitcast(FP32), ALU.subtract).then_inc(s_h2_lo, 1)
                        if u == 1:
                            normalise("A", ones + (b + 3), lambda q: y[:, (b + 2) % NRING, q, :], lambda q: k.x[:, xc(s + 2, q)], s_y)
                        if u == 2:
                            normalise("B", ones + (b + 3), lambda q: z[:, q, :], lambda q: y[:, (b + 2) % NRING, q, :], s_z)
                        mask_scores(1, (u + 1) % 2, eights + (8 * b + 2 * u + 4))
                        if u == 1:
                            weigh(2, fill + 2, fours + 4 * b)
                        if u == 0:
                            weigh(0, fill + 2, fours + 4 * b)
                        if u == 2:
                            dve.wait_ge(s_slot, fill + 2)
                            tt(flat(a_nat[:, :, :]), slot_ps[:, 0:BT], flat(y[:, (b + 3) % NRING, :, :]), ALU.add).then_inc(s_a, 1)
                            dve.wait_ge(s_a, ones + (b + 1))
                            stats("C", lambda q: a_nat[:, q, :])
                            dve.wait_ge(s_st["C"], ones + (b + 1))
                            tt(flat(xa[:, :, :]), flat(a_nat[:, :, :]), k.x[:, xc(s - 1)], ALU.add).then_inc(s_xa, 1)
                            aggregate("C")
                        phi(2 * u + 1, proj + 2, eights + (8 * b + 2 * u + QKRING + 2))
                        if u == 1:
                            dve.wait_ge(s_y, ones + (b + 3))
                            stats("B", lambda q: y[:, (b + 2) % NRING, q, :])
                            dve.wait_ge(s_st["B"], ones + (b + 3))
                            weigh(3, fill + 3, fours + 4 * b)
                            aggregate("B")
                        if u == 2:
                            normalise("C", ones + (b + 1), lambda q: an[:, q, :], lambda q: a_nat[:, q, :], s_an)
                            split_hT(ones + (b + 3), b % 2)
            n = 2 + FILLS * NB
            dve.wait_ge(s_quad, 4 * NB + 1)
            ts(den[:, :], den_ps[:, 0:BT], EPS_DEN, None, ALU.max).then_inc(s_den, 1)
            dve.wait_ge(s_den, NB + 1)
            v.reciprocal(rden[:, :], den[:, :]).then_inc(s_rden, 1)
            dve.wait_ge(s_rden, NB + 1)
            v.tensor_copy(rden_hi[:, :], rden[:, :]).then_inc(s_rhi, 1)
            dve.wait_ge(s_rhi, NB + 1)
            split_rden()
            dve.wait_ge(s_slot, n + 1)
            dve.wait_ge(s_xa, NB + 1)
            tt(k.x[:, xc(NB - 2)], slot_ps[:, 0:BT], flat(xa[:, :, :]), ALU.add).then_inc(s_x, 1)
            for i in range(UNITS):
                weigh(i, n + 2 + i, 4 * NB, s_ps[i])
            dve.wait_ge(s_slot, n + 7)
            tt(flat(a_nat[:, :, :]), slot_ps[:, 0:BT], flat(y[:, (NB - 1) % NRING, :, :]), ALU.add).then_inc(s_a, 1)
            dve.wait_ge(s_a, NB + 1)
            stats("C", lambda q: a_nat[:, q, :])
            dve.wait_ge(s_st["C"], NB + 1)
            aggregate("C")
            normalise("C", NB + 1, lambda q: an[:, q, :], lambda q: a_nat[:, q, :], s_an)
            tt(flat(xa[:, :, :]), flat(a_nat[:, :, :]), k.x[:, xc(NB - 1)], ALU.add).then_inc(s_xa, 1)
            dve.wait_ge(s_h2, NB + 1)
            v.tensor_copy(h2_hi[:, :], h2[:, :]).then_inc(s_h2_hi, 1)
            dve.wait_ge(s_h2_hi, NB + 1)
            tt(h2_lo[:, :], h2[:, :], h2_hi[:, :].bitcast(FP32), ALU.subtract).then_inc(s_h2_lo, 1)
            dve.wait_ge(s_slot, n + 11)
            dve.wait_ge(s_xa, NB + 2)
            tt(k.x[:, xc(NB - 1)], slot_ps[:, 0:BT], flat(xa[:, :, :]), ALU.add).then_inc(s_x, 1)


def macaron_kernel(nc, x, ln1_g, ln1_b, wq, wk, wv, wo, ln2_g, ln2_b, wf1, wf2,
                   rw1, rb1, rw2, rb2, we1, be1, we2, be2, out, layers=(1, 2, 3)):
    x_rows, out_rows = x.rearrange("b t d -> (b t) d"), out.rearrange("b t d -> (b t) d")
    ctx = ExitStack()
    with ctx:
        def sb(n, shape, dt=FP32):
            return ctx.enter_context(nc.sbuf_tensor(n, shape, dt))

        k = Kept()
        k.tiles = x_rows.shape[0] // TILE
        k.x = sb("x", [P, (k.tiles + 2) * TILE])
        k.raw1, k.raw2 = sb("raw1", [P, RAW, HID]), sb("raw2", [P, RAW, HC, D])
        k.rw1_hi, k.rw1_lo = sb("rw1_hi", [P, D], FP32R), sb("rw1_lo", [P, D], FP32R)
        k.rw2, k.rb2 = sb("rw2", [P, E]), sb("rb2", [P, E])
        k.cols = sb("cols", [P, ROWS])
        k.ident, k.ident_bf = sb("ident", [P, P]), sb("ident_bf", [P, P], BF16)
        k.sel = sb("sel", [SPLITS * E, E, P], BF16)
        k.earlier = sb("earlier", [P, E, E])
        k.minus_half, k.eps = sb("minus_half", [P, TQ]), sb("eps", [P, TQ])
        k.wo, k.wf2 = sb("wo", [P, AH // P, D]), sb("wf2", [P, HC, D])
        k.raw_qkv = [k.raw1[:, 0:2, :].rearrange("p a n -> p (a n)"), k.raw1[:, 2:4, :].rearrange("p a n -> p (a n)"),
                     k.raw2[:, 0:2, :, :].rearrange("p a c n -> p (a c n)")]
        k.raw_f1 = k.raw2[:, 2, :, :].rearrange("p c n -> p (c n)")

        k.n_zeroed, k.n_sel, k.n_attn_const = 9, SPLITS, 14

        def make_constants(nc, pool, zeroed):
            g = nc.gpsimd
            g.memset(k.ident[:, :], 0.0).then_inc(zeroed, 1)
            g.memset(k.minus_half[:, :], -0.5).then_inc(zeroed, 1)
            g.memset(k.eps[:, :], EPS_LN).then_inc(zeroed, 1)
            g.memset(k.ident_bf[:, :], 0.0).then_inc(zeroed, 1)
            g.memset(k.sel[:, :, :], 0.0).then_inc(zeroed, 1)
            g.memset(k.earlier[:, :, :], 1.0).then_inc(zeroed, 1)
            pool.wait_ge(zeroed, 6)
            for m in (k.ident, k.ident_bf):
                g.affine_select(out=m[:, :], in_=m[:, :], compare_op=ALU.not_equal, fill=1.0, base=0,
                                pattern=[[-1, P]], channel_multiplier=1).then_inc(zeroed, 1)
            g.affine_select(out=k.earlier[:, :, :], in_=k.earlier[:, :, :], compare_op=ALU.is_gt, fill=0.0, base=0,
                            pattern=[[1, E], [-1, E]], channel_multiplier=0).then_inc(zeroed, 1)

        def make_select(nc, pool, sel_ready):
            g = nc.gpsimd
            for part in range(SPLITS):
                if part:
                    pool.wait_ge(sel_ready, part)
                g.affine_select(out=k.sel[:, :, :], in_=k.sel[:, :, :], compare_op=ALU.not_equal, fill=1.0,
                                base=-E * part, pattern=[[-1, E], [0, P]], channel_multiplier=1).then_inc(sel_ready, 1)
            g.memset(k.x[:, 0:TILE], 0.0)
            g.memset(k.x[:, (k.tiles + 1) * TILE:(k.tiles + 2) * TILE], 0.0)

        k.make_constants, k.make_select = make_constants, make_select
        k.we1, k.we2 = we1, we2

        tile_in = [x_rows[t * TILE:(t + 1) * TILE, :].rearrange("(q p) d -> p q d", p=P) for t in range(k.tiles)]
        row = lambda a: a.rearrange("(a n) -> a n", a=1)
        loads = {
            "rows": [(slice(ROW_BE1, ROW_BE1 + E * HC), be1.rearrange("e (c p) -> (e c) p", p=P)),
                     (slice(ROW_BE2, ROW_BE2 + E), be2), (slice(ROW_RB1, ROW_RB1 + 1), row(rb1)),
                     (slice(ROW_G1, ROW_G1 + 1), row(ln1_g)), (slice(ROW_B1, ROW_B1 + 1), row(ln1_b)),
                     (slice(ROW_G2, ROW_G2 + 1), row(ln2_g)), (slice(ROW_B2, ROW_B2 + 1), row(ln2_b))],
            "rb2": row(rb2).broadcast_to([P, E]),
            "rw1": rw1, "rw2": rw2,
            "later": [(k.raw_qkv[0], wq), (k.raw_qkv[1], wk), (k.raw_qkv[2], wv), (k.raw_f1, wf1),
                      (k.wo[:, :, :], wo.rearrange("(c p) d -> p c d", p=P)), (k.wf2[:, :, :], wf2.rearrange("(c p) d -> p c d", p=P))],
        }
        ffn_phase(nc, k, "f1", x_in=tile_in, loads=loads, out=out_rows if layers == (1,) else None)
        if 2 in layers:
            attention_phase(nc, k, out=out_rows if layers == (1, 2) else None)
        if 3 in layers:
            ffn_phase(nc, k, "f2", out=out_rows)


_INS = ["L0_attn_x", "L0_attn_ln1_g", "L0_attn_ln1_b", "L0_attn_Wq", "L0_attn_Wk", "L0_attn_Wv", "L0_attn_Wo",
        "L0_attn_ln2_g", "L0_attn_ln2_b", "L0_attn_Wf1", "L0_attn_Wf2", "L0_ffn_rw1", "L0_ffn_rb1", "L0_ffn_rw2",
        "L0_ffn_rb2", "L0_ffn_we1", "L0_ffn_be1", "L0_ffn_we2", "L0_ffn_be2"]


def kernel(**inputs):
    import numpy as _np
    import concourse.bacc as _bacc
    from concourse.bass_utils import run_bass_kernel_spmd as _run

    nc = _bacc.Bacc("TRN2", target_bir_lowering=False, num_devices=1)
    arrays, args = {}, []
    for name in _INS:
        a = _np.ascontiguousarray(inputs[name])
        arrays[f"in_{name}"] = a
        args.append(nc.dram_tensor(f"in_{name}", a.shape, mybir.dt.from_np(a.dtype), kind="ExternalInput").ap())
    x = inputs["L0_attn_x"]
    args.append(nc.dram_tensor("out_x", x.shape, FP32, kind="ExternalOutput").ap())
    macaron_kernel(nc, *args)
    r = _run(nc, [arrays], core_ids=[0])
    return r.results[0]["out_x"]
```
